# Optimizing a Trainium2 kernel written in Bass

```python
import numpy as np
import jax
import jax.numpy as jnp

def _softmax(x, axis=-1):
    return jax.nn.softmax(x, axis=axis)

def _gelu(x):
    return jax.nn.gelu(x, approximate=True)

def _silu(x):
    return jax.nn.silu(x)

def _sigmoid(x):
    return jax.nn.sigmoid(x)

def _layernorm(x, axis=-1, eps=1e-05):
    m = jnp.mean(x, axis=axis, keepdims=True)
    v = jnp.var(x, axis=axis, keepdims=True)
    return (x - m) / jnp.sqrt(v + eps)

def _scatter_add(tgt, idx, src, axis=0):
    return tgt.at[idx].add(src)

def _segment_sum(src, seg, n):
    return jax.ops.segment_sum(src, seg, n)
kernel_name = 'mk_gnn_resnorm_d1_gnn_r8_727a1e'

def setup_inputs(seed: int=0):
    np.random.seed(seed)
    _w = jnp.asarray

    def _rec_inputs():
        import jax
        import jax.numpy as jnp
        _gk = jax.random.key(seed)
        x = -0.000202 + 1 * jax.random.normal(jax.random.fold_in(_gk, 1), (12500, 128), jnp.float32)
        _s = jax.random.randint(jax.random.fold_in(_gk, 2), (100000,), 0, 12500, jnp.int32)
        _d = jax.random.randint(jax.random.fold_in(_gk, 3), (100000,), 0, 12500, jnp.int32)
        _loop = jnp.arange(12500, dtype=jnp.int32)
        src = jnp.concatenate([_s, _d, _loop])
        dst = jnp.concatenate([_d, _s, _loop])
        _o = jnp.argsort(dst, stable=True)
        src = src[_o]
        dst = dst[_o]
        edge_attr_16 = 0.00028786 + 0.999816 * jax.random.normal(jax.random.fold_in(_gk, 11), (212500, 16), jnp.float32)
        return (x, src, dst, edge_attr_16)
    x, src, dst, edge_attr_16 = _rec_inputs()

    def _L0_gnn_setup():
        import jax, jax.numpy as jnp
        import numpy as np
        BN_EPS = 1e-05

        def _bn(x, gamma, beta):
            m = jnp.mean(x, axis=0)
            v = jnp.var(x, axis=0)
            return (x - m) * jax.lax.rsqrt(v + BN_EPS) * gamma + beta
        key = jax.random.key(seed)
        ks = jax.random.split(key, 12)
        N, E, D, ED = (6250, 75000, 128, 16)
        s = lambda k, sh: jax.random.normal(k, sh, dtype=jnp.float32) * 0.05
        return {'h': jax.random.normal(ks[0], (N, D), dtype=jnp.float32), 'edge_index': jax.random.randint(ks[1], (2, E), 0, N, dtype=jnp.int64), 'edge_attr': jax.random.normal(ks[2], (E, ED), dtype=jnp.float32), 'ee_w1': s(ks[3], (ED, D)), 'ee_b1': jnp.zeros((D,), jnp.float32), 'ee_g1': jnp.ones((D,), jnp.float32), 'ee_bb1': jnp.zeros((D,), jnp.float32), 'ee_w2': s(ks[4], (D, D)), 'ee_b2': jnp.zeros((D,), jnp.float32), 'mlp_w1': s(ks[5], (D, D)), 'mlp_b1': jnp.zeros((D,), jnp.float32), 'mlp_g1': jnp.ones((D,), jnp.float32), 'mlp_bb1': jnp.zeros((D,), jnp.float32), 'mlp_w2': s(ks[6], (D, D)), 'mlp_b2': jnp.zeros((D,), jnp.float32), 'mlp_g2': jnp.ones((D,), jnp.float32), 'mlp_bb2': jnp.zeros((D,), jnp.float32)}
    _L0_gnn_all = _L0_gnn_setup()
    _L0_gnn_in = {k: v for k, v in _L0_gnn_all.items() if k in ('ee_w1', 'ee_b1', 'ee_g1', 'ee_bb1', 'ee_w2', 'ee_b2', 'mlp_w1', 'mlp_b1', 'mlp_g1', 'mlp_bb1', 'mlp_w2', 'mlp_b2', 'mlp_g2', 'mlp_bb2')}
    del _L0_gnn_all
    return {'x': x, 'src': src, 'dst': dst, 'edge_attr_16': edge_attr_16, 'L0_gnn_ee_w1': _L0_gnn_in['ee_w1'], 'L0_gnn_ee_b1': _L0_gnn_in['ee_b1'], 'L0_gnn_ee_g1': _L0_gnn_in['ee_g1'], 'L0_gnn_ee_bb1': _L0_gnn_in['ee_bb1'], 'L0_gnn_ee_w2': _L0_gnn_in['ee_w2'], 'L0_gnn_ee_b2': _L0_gnn_in['ee_b2'], 'L0_gnn_mlp_w1': _L0_gnn_in['mlp_w1'], 'L0_gnn_mlp_b1': _L0_gnn_in['mlp_b1'], 'L0_gnn_mlp_g1': _L0_gnn_in['mlp_g1'], 'L0_gnn_mlp_bb1': _L0_gnn_in['mlp_bb1'], 'L0_gnn_mlp_w2': _L0_gnn_in['mlp_w2'], 'L0_gnn_mlp_b2': _L0_gnn_in['mlp_b2'], 'L0_gnn_mlp_g2': _L0_gnn_in['mlp_g2'], 'L0_gnn_mlp_bb2': _L0_gnn_in['mlp_bb2']}

def reference(x, src, dst, edge_attr_16, L0_gnn_ee_w1, L0_gnn_ee_b1, L0_gnn_ee_g1, L0_gnn_ee_bb1, L0_gnn_ee_w2, L0_gnn_ee_b2, L0_gnn_mlp_w1, L0_gnn_mlp_b1, L0_gnn_mlp_g1, L0_gnn_mlp_bb1, L0_gnn_mlp_w2, L0_gnn_mlp_b2, L0_gnn_mlp_g2, L0_gnn_mlp_bb2):
    import jax
    import jax.numpy as jnp

    def _L0_gnn_ref(h, edge_index, edge_attr, ee_w1, ee_b1, ee_g1, ee_bb1, ee_w2, ee_b2, mlp_w1, mlp_b1, mlp_g1, mlp_bb1, mlp_w2, mlp_b2, mlp_g2, mlp_bb2):
        import jax, jax.numpy as jnp
        import numpy as np
        BN_EPS = 1e-05

        def _bn(x, gamma, beta):
            m = jnp.mean(x, axis=0)
            v = jnp.var(x, axis=0)
            return (x - m) * jax.lax.rsqrt(v + BN_EPS) * gamma + beta
        N = h.shape[0]
        src, dst = (edge_index[0], edge_index[1])
        e = jax.nn.relu(_bn(edge_attr @ ee_w1 + ee_b1, ee_g1, ee_bb1)) @ ee_w2 + ee_b2
        agg_edge = jax.ops.segment_sum(e, dst, num_segments=N)
        h = h + agg_edge
        neigh = jax.ops.segment_sum(h[src], dst, num_segments=N)
        z = h + neigh
        z = jax.nn.relu(_bn(z @ mlp_w1 + mlp_b1, mlp_g1, mlp_bb1))
        z = jax.nn.relu(_bn(z @ mlp_w2 + mlp_b2, mlp_g2, mlp_bb2))
        return z
    edge_index = jnp.stack([src, dst])
    x = _layernorm(x + _L0_gnn_ref(x, edge_index, edge_attr_16, L0_gnn_ee_w1, L0_gnn_ee_b1, L0_gnn_ee_g1, L0_gnn_ee_bb1, L0_gnn_ee_w2, L0_gnn_ee_b2, L0_gnn_mlp_w1, L0_gnn_mlp_b1, L0_gnn_mlp_g1, L0_gnn_mlp_bb1, L0_gnn_mlp_w2, L0_gnn_mlp_b2, L0_gnn_mlp_g2, L0_gnn_mlp_bb2), axis=-1)
    return x

_drawn_inputs = setup_inputs


def setup_inputs(seed=0):
    import zlib

    import numpy as np

    out = dict(_drawn_inputs(seed))
    spreads = {'L0_gnn_ee_b1': (0.0, 0.1),
     'L0_gnn_ee_g1': (1.0, 0.2),
     'L0_gnn_ee_bb1': (0.0, 0.1),
     'L0_gnn_ee_b2': (0.0, 0.1),
     'L0_gnn_mlp_b1': (0.0, 0.1),
     'L0_gnn_mlp_g1': (1.0, 0.2),
     'L0_gnn_mlp_bb1': (0.0, 0.1),
     'L0_gnn_mlp_b2': (0.0, 0.1),
     'L0_gnn_mlp_g2': (1.0, 0.2),
     'L0_gnn_mlp_bb2': (0.0, 0.1)}
    factors = {}
    for name, (base, spread) in spreads.items():
        noise = np.random.default_rng([zlib.crc32(name.encode()), seed]).standard_normal(out[name].shape)
        drawn = base * np.exp(spread * noise) if base else spread * noise
        out[name] = jnp.asarray(drawn.astype(out[name].dtype))
    for name, factor in factors.items():
        out[name] = (out[name] * factor).astype(out[name].dtype)
    return out
```

```python
from contextlib import ExitStack

import numpy as np
import concourse.bass as bass
from concourse import mybir

F32, I32, BF16 = mybir.dt.float32, mybir.dt.int32, mybir.dt.bfloat16
ALU = mybir.AluOpType
ACT = mybir.ActivationFunctionType
AX_X = mybir.AxisListType.X

P = 128
N, E, D, ED = 12500, 212500, 128, 16
EPS = 1e-5
GROUP_TILES = 8
GROUP_EDGES = GROUP_TILES * P
GROUPS = -(-E // GROUP_EDGES)
TILES = GROUPS * GROUP_TILES
WINDOW = 96
ROUNDS_ALL = -(-N // WINDOW)
NT = ROUNDS_ALL * WINDOW + WINDOW
NO_NODE = 1 << 20
QUAD = 4
BODY = 4
BODIES = GROUPS // BODY
EA_COLS = 2 * GROUP_EDGES // QUAD
GRAM_COLS, GRAM_SLOTS = 512, 4
GRAM_LOADS = TILES * ED // GRAM_COLS
GRAM_BODIES = GRAM_LOADS // GRAM_SLOTS
CHUNK = 512
CHUNKS = N // CHUNK
TAIL = N - CHUNKS * CHUNK
PER = 4
BASE_ROWS = GROUPS // 2

assert GROUPS % BODY == 0 and GRAM_LOADS % GRAM_SLOTS == 0 and CHUNKS % 2 == 0 and TAIL % PER == 0


def wait(engine, semaphore, value):
    if isinstance(value, int) and value <= 0:
        return
    engine.wait_ge(semaphore, value)


def inverse_root(pool, out, variance, eps, minus_half, semaphore, value):
    pool.tensor_tensor(out, variance, eps, ALU.add).then_inc(semaphore, 1)
    pool.wait_ge(semaphore, value)
    pool.tensor_tensor(out, out, minus_half, ALU.pow).then_inc(semaphore, 1)


def build(nc, a):
    with ExitStack() as ctx:
        def sb(name, shape, dt=F32):
            return ctx.enter_context(nc.sbuf_tensor(name, shape, dt))

        def sem(name):
            return ctx.enter_context(nc.semaphore(name))

        table = sb("table", [P, 2, NT])
        rows = sb("rows", [P, 4, GROUP_TILES * D])
        onehot = sb("onehot", [P, 2, GROUP_TILES, WINDOW])
        ea = sb("ea", [P, 2, EA_COLS])
        dst_i = sb("dst_i", [P, TILES], I32)
        dst_f = sb("dst_f", [P, TILES])
        rel = sb("rel", [P, TILES])
        idx = sb("idx", [P, 2, 2 * GROUP_TILES], I32)
        iota = sb("iota_sb", [P, WINDOW])
        ident = sb("ident_sb", [P, P])
        block_mask = sb("block_mask_sb", [P, P])
        fold = sb("fold_sb", [P, ED])
        ones = sb("ones", [P, P])
        minus_half = sb("minus_half", [P, D])
        eps = sb("eps", [P, D])
        ones_bf = sb("ones_bf", [P, P], BF16)
        ee_w1bd = sb("ee_w1bd_sb", [4 * ED, QUAD * D])
        ee_w1f = sb("ee_w1f", [P, QUAD * D])
        ee_w1 = sb("ee_w1_sb", [ED, D])
        ee_w2 = sb("ee_w2_sb", [D, D])
        mlp_w1 = sb("mlp_w1_sb", [D, D])
        mlp_w2 = sb("mlp_w2_sb", [D, D])
        rowvec = sb("rowvec", [P, 3, D])
        colvec = sb("colvec", [P, 7])
        stage_x = sb("stage_x", [P, 2, CHUNK])
        stage_h = sb("stage_h", [P, 2, CHUNK])
        stage_o = sb("stage_o", [P, 2, CHUNK])
        part = sb("part", [P, GRAM_LOADS, ED])
        part1 = sb("part1", [P, ED])
        gram = sb("gram", [P, P])
        gram1 = sb("gram1", [P, ED])
        mean_row = sb("mean_row", [1, ED])
        mean_col = sb("mean_col", [ED, 1])
        cov = sb("cov", [ED, ED])
        cov1 = sb("cov1", [ED, ED])
        prod = sb("prod", [ED, 2, D])
        bnrow = sb("bnrow", [P, 5, D])
        base_min = sb("base_min", [BASE_ROWS, 2])
        base0 = sb("base0", [P, GROUPS])
        base = sb("base", [P, GROUPS])
        base_i = sb("base_i", [1, GROUPS], I32)
        wide = sb("wide", [P, 4])
        rounds_i = sb("rounds_i", [1, 1], I32)
        bn_parts = sb("bn_parts", [P, CHUNKS + 1, 6])
        bn_out = sb("bn_out", [P, 2, 2])
        bn_col = sb("bn_col", [P, 2, 4])
        ln_parts = sb("ln_parts", [P, 2, PER, 6])
        ln_out = sb("ln_out", [P, 2, PER, 2])
        ln_rstd = sb("ln_rstd", [P, 2, PER])
        ps = ctx.enter_context(nc.psum_tensor("ps", [P, 8, 512], F32))

        base_dram = nc.dram_tensor("base_scratch", (GROUPS,), F32, kind="Internal").ap()
        h_dram = nc.dram_tensor("h_scratch", (N, D), F32, kind="Internal").ap()

        weights_in, dst_in, groups_in, base_out, base_in = (
            sem(n) for n in ("weights_in", "dst_in", "groups_in", "base_out", "base_in"))
        gram_in = [sem(f"gram_in{s}") for s in range(GRAM_SLOTS)]
        gram_summed, gram_done = sem("gram_summed"), sem("gram_done")
        base_ready, step, pe_step, cleared = sem("base_ready"), sem("step"), sem("pe_step"), sem("cleared")
        root_ready = sem("root_ready")
        WEIGHTS = 12 + 7

        with nc.Block() as block:
            @block.sync
            def _(sp):
                sp.dma_start(table[0:BASE_ROWS, 1, 0:2 * GROUP_EDGES].bitcast(I32),
                             a["dst_groups"].rearrange("(r two) e -> r (two e)", two=2)).then_inc(groups_in, 16)
                sp.dma_start(dst_i[:], a["dst_tiles"]).then_inc(dst_in, 16)

                def load(s, n):
                    sp.dma_start(rows[:, s, 0:GRAM_COLS],
                                 a["edges"][:, bass.ds(n * GRAM_COLS, GRAM_COLS)]).then_inc(gram_in[s], 16)
                for s in range(GRAM_SLOTS):
                    load(s, s)
                with sp.Fori(1, GRAM_BODIES) as i:
                    for s in range(GRAM_SLOTS):
                        sp.wait_ge(gram_done, i * GRAM_SLOTS + (s + 1 - GRAM_SLOTS))
                        sp.wait_ge(gram_summed, i * GRAM_SLOTS + (s + 1 - GRAM_SLOTS))
                        load(s, i * GRAM_SLOTS + s)

            @block.scalar
            def _(act):
                for t, n in ((ident, "ident"), (iota, "iota"), (block_mask, "block_mask"), (fold, "fold"),
                             (ee_w1bd, "ee_w1bd"), (ee_w1, "ee_w1"), (ee_w2, "ee_w2"),
                             (mlp_w1, "mlp_w1"), (mlp_w2, "mlp_w2")):
                    act.dma_start(t[:], a[n]).then_inc(weights_in, 16)
                for k, n in enumerate(("ee_b1", "ee_g1", "ee_bb1")):
                    act.dma_start(rowvec[:, k, :], a[n].rearrange("(o d) -> o d", o=1).broadcast_to([P, D])
                                  ).then_inc(weights_in, 16)
                for k, n in enumerate(("ee_b2", "mlp_b1", "mlp_g1", "mlp_bb1", "mlp_b2", "mlp_g2", "mlp_bb2")):
                    act.dma_start(colvec[:, k:k + 1], a[n].rearrange("(d o) -> d o", o=1)).then_inc(weights_in, 16)
                act.wait_ge(base_ready, 1)
                act.dma_start(base_dram.rearrange("(r two) -> r two", two=2), base_min[:]).then_inc(base_out, 16)
                act.wait_ge(base_out, 16)
                act.dma_start(base0[:], base_dram.rearrange("(o g) -> o g", o=1).broadcast_to([P, GROUPS])
                              ).then_inc(base_in, 16)

            @block.gpsimd
            def _(pool):
                pool.memset(ones[:], 1.0).then_inc(cleared, 1)
                pool.memset(ones_bf[:], 1.0).then_inc(cleared, 1)
                pool.memset(minus_half[:], -0.5).then_inc(cleared, 1)
                pool.memset(eps[:], EPS).then_inc(cleared, 1)
                pool.memset(table[:, 0, :], 0.0).then_inc(cleared, 1)
                pool.wait_ge(base_ready, 1)
                pool.memset(table[:, 1, :], 0.0).then_inc(cleared, 1)
                pool.wait_ge(step, 10)
                pool.wait_ge(cleared, 4)
                inverse_root(pool, bnrow[:, 0, :], bnrow[:, 2, :], eps[:], minus_half[:], root_ready, 1)

            @block.tensor
            def _(pe):
                def gram_slot(n, s, i):
                    pe.wait_ge(gram_in[s], 16 * (i + 1))
                    for b in range(GRAM_COLS // P):
                        x = rows[:, s, b * P:(b + 1) * P]
                        mm = pe.matmul(ps[:, 0, 0:P], x, x, start=(n == 0 and b == 0), stop=True,
                                       skip_group_check=True)
                    mm.then_inc(gram_done, 1)
                for s in range(GRAM_SLOTS):
                    gram_slot(s, s, 0)
                with pe.Fori(1, GRAM_BODIES) as i:
                    for s in range(GRAM_SLOTS):
                        gram_slot(None, s, i)
                pe.wait_ge(cleared, 1)
                pe.wait_ge(step, 2)
                pe.wait_ge(weights_in, 16 * WEIGHTS)
                pe.matmul(ps[0:1, 1, 0:ED], ones[:, 0:1], part1[:], start=True, stop=True)
                pe.matmul(ps[0:ED, 2, 0:1], part1[:], ones[:, 0:1], start=True, stop=True)
                pe.matmul(ps[:, 3, 0:ED], gram[:], fold[:], start=True, stop=True).then_inc(pe_step, 1)
                pe.wait_ge(step, 5)
                pe.matmul(ps[0:ED, 4, 0:ED], fold[:], gram1[:], start=True, stop=True)
                pe.matmul(ps[0:ED, 5, 0:ED], mean_row[:], mean_row[:], start=True, stop=True).then_inc(pe_step, 1)
                pe.wait_ge(step, 7)
                pe.matmul(ps[0:ED, 6, 0:D], cov[:], ee_w1[:], start=True, stop=True).then_inc(pe_step, 1)
                pe.wait_ge(step, 9)
                pe.matmul(ps[:, 7, 0:D], ones[0:ED, :], prod[:, 0, :], start=True, stop=True)
                pe.matmul(ps[:, 7, D:2 * D], ones[0:ED, :], prod[:, 1, :], start=True, stop=True
                          ).then_inc(pe_step, 1)
                pe.wait_ge(step, 18)
                pe.matmul(ps[:, 1, 0:1], ones[:], wide[:, 0:1], start=True, stop=True).then_inc(pe_step, 1)

            @block.vector
            def _(dve):
                steps = [0]

                def link(ins):
                    steps[0] += 1
                    ins.then_inc(step, 1)
                    dve.wait_ge(step, steps[0])

                dve.memset(ea[QUAD * ED:QUAD * ED + 1, :, :], 1.0)
                dve.wait_ge(groups_in, 16)
                dve.tensor_reduce(base_min[:], table[0:BASE_ROWS, 1, 0:2 * GROUP_EDGES].bitcast(I32)
                                  .rearrange("r (two e) -> r two e", two=2), AX_X, ALU.min).then_inc(base_ready, 1)
                dve.wait_ge(dst_in, 16)
                dve.tensor_copy(dst_f[:], dst_i[:]).then_inc(base_ready, 1)

                def sum_slot(s, i):
                    dve.wait_ge(gram_in[s], 16 * (i + 1))
                    dve.tensor_reduce(part[:, bass.ds(i * GRAM_SLOTS + s, 1), :],
                                      rows[:, s, 0:GRAM_COLS].rearrange("p (n c) -> p c n", c=ED),
                                      AX_X, ALU.add).then_inc(gram_summed, 1)
                with dve.Fori(0, GRAM_BODIES) as i:
                    for s in range(GRAM_SLOTS):
                        sum_slot(s, i)
                dve.wait_ge(gram_summed, GRAM_LOADS)
                link(dve.tensor_reduce(part1[:], part[:].rearrange("p n c -> p c n"), AX_X, ALU.add))
                dve.wait_ge(gram_done, GRAM_LOADS)
                dve.wait_ge(weights_in, 16 * WEIGHTS)
                link(dve.tensor_tensor(gram[:], ps[:, 0, 0:P], block_mask[:], ALU.mult))
                dve.wait_ge(pe_step, 1)
                link(dve.tensor_scalar(mean_row[:], ps[0:1, 1, 0:ED], 1.0 / E, None, ALU.mult))
                link(dve.tensor_scalar(mean_col[:], ps[0:ED, 2, 0:1], 1.0 / E, None, ALU.mult))
                link(dve.tensor_copy(gram1[:], ps[:, 3, 0:ED]))
                dve.wait_ge(pe_step, 2)
                link(dve.tensor_scalar(cov1[:], ps[0:ED, 4, 0:ED], 1.0 / E, None, ALU.mult))
                link(dve.tensor_tensor(cov[:], cov1[:], ps[0:ED, 5, 0:ED], ALU.subtract))
                dve.wait_ge(pe_step, 3)
                link(dve.tensor_tensor(prod[:, 0, :], ps[0:ED, 6, 0:D], ee_w1[:], ALU.mult))
                link(dve.tensor_scalar(prod[:, 1, :], ee_w1[:], mean_col[:, 0:1], None, ALU.mult))
                dve.wait_ge(pe_step, 4)
                link(dve.tensor_copy(bnrow[:, 2, :], ps[:, 7, 0:D]))
                dve.wait_ge(root_ready, 2)
                link(dve.tensor_tensor(bnrow[:, 1, :], bnrow[:, 0, :], rowvec[:, 1, :], ALU.mult))
                link(dve.tensor_tensor(bnrow[:, 2, :], ps[:, 7, D:2 * D], rowvec[:, 0, :], ALU.add))
                link(dve.tensor_tensor(bnrow[:, 3, :], rowvec[:, 0, :], bnrow[:, 2, :], ALU.subtract))
                link(dve.tensor_tensor(bnrow[:, 4, :], bnrow[:, 3, :], bnrow[:, 1, :], ALU.mult))
                dve.tensor_tensor(ee_w1f[0:4 * ED, :].rearrange("r (q d) -> r q d", q=QUAD),
                                  ee_w1bd[:].rearrange("r (q d) -> r q d", q=QUAD),
                                  bnrow[0:4 * ED, 1:2, :].broadcast_to([4 * ED, QUAD, D]), ALU.mult)
                dve.tensor_tensor(ee_w1f[64:65, :].rearrange("r (q d) -> r q d", q=QUAD),
                                  bnrow[64:65, 4:5, :].broadcast_to([1, QUAD, D]),
                                  rowvec[64:65, 2:3, :].broadcast_to([1, QUAD, D]), ALU.add)

                dve.wait_ge(base_in, 16)
                dve.wait_ge(base_ready, 2)
                link(dve.tensor_tensor(rel[:].rearrange("p (g t) -> p g t", t=GROUP_TILES),
                                       dst_f[:].rearrange("p (g t) -> p g t", t=GROUP_TILES),
                                       base0[:].unsqueeze(2).broadcast_to([P, GROUPS, GROUP_TILES]), ALU.subtract))
                link(dve.tensor_scalar(dst_i[:].bitcast(F32), rel[:], NO_NODE / 2.0, None, ALU.is_lt))
                link(dve.scalar_tensor_tensor(rel[:], rel[:], float(WINDOW), dst_i[:].bitcast(F32),
                                              ALU.is_ge, ALU.mult))
                ins = dve.tensor_reduce(wide[:, 0:1], rel[:], AX_X, ALU.max)
                steps[0] += 1
                ins.then_inc(step, 1)
                dve.wait_ge(pe_step, 5)
                link(dve.tensor_scalar(wide[:, 1:2], ps[:, 1, 0:1], 0.5, None, ALU.is_ge))
                link(dve.tensor_scalar(wide[:, 2:3], wide[:, 1:2], -1.0, 1.0, ALU.mult, ALU.add))
                link(dve.tensor_scalar(rounds_i[:], wide[0:1, 1:2], float(ROUNDS_ALL - 1), 1.0, ALU.mult, ALU.add))

        ea_in = [sem("ea_in0"), sem("ea_in1")]
        features_done, relu_done, onehot_done, sums_done, added = (
            sem(n) for n in ("features_done", "relu_done", "onehot_done", "sums_done", "added"))
        idx_in = [sem("idx_in0"), sem("idx_in1")]
        gathering = sem("gathering")
        gathered = [sem(f"gathered{s}") for s in range(4)]
        round_sems = [*ea_in, features_done, relu_done, onehot_done, sums_done, added, *idx_in, gathering, *gathered]

        def rewind():
            with nc.Block() as block:
                @block.vector
                def _(dve):
                    dve.tensor_scalar(base[:], base0[:], wide[:, 2:3], None, ALU.mult)

        def open_round():
            with nc.Block() as block:
                @block.gpsimd
                def _(pool):
                    for s in round_sems:
                        pool.sem_clear(s)

                @block.vector
                def _(dve):
                    dve.tensor_tensor(rel[:].rearrange("p (g t) -> p g t", t=GROUP_TILES),
                                      dst_f[:].rearrange("p (g t) -> p g t", t=GROUP_TILES),
                                      base[:].unsqueeze(2).broadcast_to([P, GROUPS, GROUP_TILES]), ALU.subtract)
                    dve.tensor_copy(base_i[:], base[0:1, :])

        def window_sums(dve, kinds):
            def make_onehot(g, u):
                wait(dve, sums_done, g - 1)
                dve.tensor_tensor(onehot[:, u % 2],
                                  iota[:].unsqueeze(1).broadcast_to([P, GROUP_TILES, WINDOW]),
                                  rel[:, bass.ds(g * GROUP_TILES, GROUP_TILES)].unsqueeze(2)
                                  .broadcast_to([P, GROUP_TILES, WINDOW]), ALU.is_equal).then_inc(onehot_done, 1)

            def add_window(g, u):
                at = dve.value_load(base_i[0:1, bass.ds(g, 1)], min_val=0, max_val=NT - WINDOW)
                dve.wait_ge(sums_done, g + 1)
                wait(dve, added, g)
                here = table[:, 0:kinds, bass.ds(at, WINDOW)]
                dve.tensor_tensor(here, here, ps[:, 4 + 2 * (u % 2):4 + 2 * (u % 2) + kinds, 0:WINDOW], ALU.add
                                  ).then_inc(added, 1)

            def body(i, last=False):
                for u in range(BODY):
                    if not (last and u == BODY - 1):
                        make_onehot(i * BODY + u + 1, u + 1)
                    add_window(i * BODY + u, u)

            make_onehot(0, 0)
            body(0)
            with dve.Fori(1, BODIES - 1) as i:
                body(i)
            body(BODIES - 1, last=True)
            dve.tensor_scalar(base[:], base[:], float(WINDOW), None, ALU.add)

        rewind()
        nc.all_engine_barrier()
        rounds = nc.values_load(rounds_i[0:1, 0:1], min_val=1, max_val=ROUNDS_ALL)
        with nc.Fori(0, rounds):
            open_round()
            with nc.Block() as block:
                @block.sync
                def _(sp):
                    def load(i, s):
                        sp.dma_start(ea[0:QUAD * ED, s, :],
                                     a["edges_t"][:, bass.ds((i * 2 + s) * EA_COLS, EA_COLS)]).then_inc(ea_in[s], 16)
                    load(0, 0)
                    load(0, 1)
                    with sp.Fori(1, BODIES) as i:
                        for s in range(2):
                            sp.wait_ge(features_done, i * (2 * BODY) + (4 * s - 4))
                            load(i, s)

                @block.tensor
                def _(pe):
                    def features(i, u):
                        if u == BODY:
                            i, u = i + 1, 0
                        g = i * BODY + u
                        if u % 2 == 0:
                            pe.wait_ge(ea_in[u // 2], 16 * (i + 1))
                        for half in range(2):
                            wait(pe, relu_done, 2 * g + (half - 3))
                            c = ((u % 2) * 2 + half) * P
                            pe.matmul(ps[:, 2 * (u % 2) + half, :], ea[0:QUAD * ED + 1, u // 2, c:c + P],
                                      ee_w1f[0:QUAD * ED + 1, :], start=True, stop=True).then_inc(features_done, 1)

                    def sums(i, u):
                        g = i * BODY + u
                        wait(pe, added, g - 1)
                        pe.wait_ge(onehot_done, g + 1)
                        pe.wait_ge(relu_done, 2 * g + 2)
                        for t in range(GROUP_TILES):
                            pe.matmul(ps[:, 4 + 2 * (u % 2), 0:WINDOW], rows[:, u % 2, t * D:(t + 1) * D],
                                      onehot[:, u % 2, t, :], start=(t == 0), stop=(t == GROUP_TILES - 1))
                        for t in range(GROUP_TILES):
                            mm = pe.matmul(ps[:, 5 + 2 * (u % 2), 0:WINDOW], ones_bf[:],
                                           onehot[:, u % 2, t, :].bitcast(BF16)[:, 1:2 * WINDOW:2],
                                           start=(t == 0), stop=(t == GROUP_TILES - 1))
                        mm.then_inc(sums_done, 1)

                    def body(i, last=False):
                        for u in range(BODY):
                            if not (last and u == BODY - 1):
                                features(i, u + 1)
                            sums(i, u)

                    features(0, 0)
                    body(0)
                    with pe.Fori(1, BODIES - 1) as i:
                        body(i)
                    body(BODIES - 1, last=True)

                @block.scalar
                def _(act):
                    def body(i):
                        for u in range(BODY):
                            g = i * BODY + u
                            for half in range(2):
                                wait(act, sums_done, g - 1)
                                act.wait_ge(features_done, 2 * g + half + 1)
                                act.activation(rows[:, u % 2, half * 512:(half + 1) * 512],
                                               ps[:, 2 * (u % 2) + half, :], ACT.Relu).then_inc(relu_done, 1)
                    body(0)
                    with act.Fori(1, BODIES) as i:
                        body(i)

                @block.vector
                def _(dve):
                    window_sums(dve, kinds=2)

        x_in, h_out = [sem("x_in0"), sem("x_in1")], [sem("h_out0"), sem("h_out1")]
        projected, h_half, h_ready, h_kept, turned, h_copied = (
            sem(n) for n in ("projected", "h_half", "h_ready", "h_kept", "turned", "h_copied"))

        def over_chunks(engine, step_of, first=0):
            for s in range(2):
                step_of(s, s, CHUNK)
            with engine.Fori(1, CHUNKS // 2) as i:
                for s in range(2):
                    step_of(i * 2 + s, s, CHUNK)
            step_of(CHUNKS, CHUNKS % 2, TAIL)

        def turn(pe, bank, source, n):
            for k in range(PER):
                tr = pe.transpose(ps[0:n // PER, bank, k * D:(k + 1) * D], source[:, k:n:PER], ident[:])
            return tr

        def rows_of(dram, c, n):
            return dram[bass.ds(c * CHUNK, n), :].rearrange("(p k) d -> p (k d)", k=PER)

        with nc.Block() as block:
            @block.sync
            def _(sp):
                def load(c, s, n):
                    wait(sp, h_ready, c - 1)
                    sp.dma_start(stage_x[:, s, 0:n], a["x_t"][:, bass.ds(c * CHUNK, n)]).then_inc(x_in[s], 16)
                over_chunks(sp, load)

            @block.gpsimd
            def _(pool):
                def store(c, s, n):
                    pool.wait_ge(h_copied, c + 1)
                    pool.dma_start(rows_of(h_dram, c, n), stage_o[0:n // PER, s, :]).then_inc(h_out[s], 16)
                over_chunks(pool, store)
                pool.wait_ge(h_out[0], 16 * (CHUNKS // 2 + 1))
                pool.wait_ge(h_out[1], 16 * (CHUNKS // 2))

            @block.tensor
            def _(pe):
                def project(c, s, n):
                    wait(pe, h_half, c - 1)
                    pe.matmul(ps[:, s, 0:n], ee_w2[:], table[:, 0, bass.ds(c * CHUNK, n)], start=True, stop=True
                              ).then_inc(projected, 1)
                    pe.wait_ge(h_ready, c + 1)
                    wait(pe, h_copied, c - 1)
                    turn(pe, 2 + s, stage_h[:, s, :], n).then_inc(turned, 1)
                over_chunks(pe, project)

            @block.vector
            def _(dve):
                def combine(c, s, n):
                    dve.wait_ge(projected, c + 1)
                    wait(dve, turned, c - 1)
                    wait(dve, h_kept, c - 1)
                    dve.scalar_tensor_tensor(stage_h[:, s, 0:n], table[:, 1, bass.ds(c * CHUNK, n)], colvec[:, 0:1],
                                             ps[:, s, 0:n], ALU.mult, ALU.add).then_inc(h_half, 1)
                    dve.wait_ge(x_in[s], 16 * (c // 2 + 1) if isinstance(c, int) else (c + (2 - s)) * 8)
                    dve.wait_ge(h_half, c + 1)
                    dve.tensor_tensor(stage_h[:, s, 0:n], stage_h[:, s, 0:n], stage_x[:, s, 0:n], ALU.add
                                      ).then_inc(h_ready, 1)
                over_chunks(dve, combine)

            @block.scalar
            def _(act):
                def keep(c, s, n):
                    act.wait_ge(h_ready, c + 1)
                    act.copy(table[:, 0, bass.ds(c * CHUNK, n)], stage_h[:, s, 0:n]).then_inc(h_kept, 1)
                    act.wait_ge(turned, c + 1)
                    if isinstance(c, int):
                        wait(act, h_out[s], 16 * (c // 2))
                    else:
                        act.wait_ge(h_out[s], (c - s) * 8)
                    act.copy(stage_o[0:n // PER, s, :], ps[0:n // PER, 2 + s, :]).then_inc(h_copied, 1)
                over_chunks(act, keep)

        rewind()
        with nc.Fori(0, rounds):
            open_round()
            with nc.Block() as block:
                @block.sync
                def _(sp):
                    def load(i, s):
                        sp.dma_start(idx[:, s, :], a["src_tiles"][:, bass.ds((i * 2 + s) * 2 * GROUP_TILES,
                                                                             2 * GROUP_TILES)]).then_inc(idx_in[s], 16)
                    load(0, 0)
                    load(0, 1)
                    with sp.Fori(1, BODIES) as i:
                        for s in range(2):
                            sp.wait_ge(gathered[2 * s], i * (16 * GROUP_TILES))
                            sp.wait_ge(gathered[2 * s + 1], i * (16 * GROUP_TILES))
                            load(i, s)

                @block.gpsimd
                def _(pool):
                    def body(i):
                        for u in range(BODY):
                            if u % 2 == 0:
                                pool.wait_ge(idx_in[u // 2], 16 * (i + 1))
                            wait(pool, sums_done, i * BODY + (u - 3))
                            pool.sem_inc(gathering, 1)
                            for t in range(GROUP_TILES):
                                k = (u % 2) * GROUP_TILES + t
                                pool.indirect_dma_start(
                                    rows[:, u, t * D:(t + 1) * D], None, h_dram,
                                    bass.IndirectOffsetOnAxis(ap=idx[:, u // 2, k:k + 1], axis=0)
                                ).then_inc(gathered[u], 16)
                    body(0)
                    with pool.Fori(1, BODIES) as i:
                        body(i)

                @block.tensor
                def _(pe):
                    def body(i):
                        for u in range(BODY):
                            g = i * BODY + u
                            wait(pe, added, g - 1)
                            pe.wait_ge(onehot_done, g + 1)
                            pe.wait_ge(gathered[u], (i + 1) * (16 * GROUP_TILES))
                            for t in range(GROUP_TILES):
                                mm = pe.matmul(ps[:, 4 + 2 * (u % 2), 0:WINDOW], rows[:, u, t * D:(t + 1) * D],
                                               onehot[:, u % 2, t, :], start=(t == 0), stop=(t == GROUP_TILES - 1))
                            mm.then_inc(sums_done, 1)
                    body(0)
                    with pe.Fori(1, BODIES) as i:
                        body(i)

                @block.vector
                def _(dve):
                    window_sums(dve, kinds=1)

        made, kept, stats, ready, bn_root = ([sem(f"{n}{k}") for k in range(2)]
                                    for n in ("made", "kept", "stats", "bn_ready", "bn_root"))
        relued = sem("relued")
        z, y1, y2 = table[:, 0], table[:, 1], table[:, 0]
        for layer in range(2):
            weight, bias = (mlp_w1, 1) if layer == 0 else (mlp_w2, 4)
            source, out = (z, y1) if layer == 0 else (y1, y2)
            with nc.Block() as block:
                @block.gpsimd
                def _(pool, layer=layer):
                    pool.wait_ge(ready[layer], 1)
                    inverse_root(pool, bn_col[:, layer, 0:1], bn_out[:, layer, 1:2], eps[:, 0:1], minus_half[:, 0:1],
                                 bn_root[layer], 1)

                @block.tensor
                def _(pe, layer=layer, weight=weight, source=source):
                    def dense(c, s, n):
                        wait(pe, kept[layer], c - 1)
                        if layer:
                            pe.wait_ge(relued, c + 1)
                        moving = stage_h[:, s, 0:n] if layer else source[:, bass.ds(c * CHUNK, n)]
                        pe.matmul(ps[:, s, 0:n], weight[:], moving, start=True, stop=True).then_inc(made[layer], 1)
                    over_chunks(pe, dense)

                @block.scalar
                def _(act, layer=layer, bias=bias, source=source, out=out):
                    def keep(c, s, n):
                        if layer:
                            wait(act, made[1], c - 1)
                            act.activation(stage_h[:, s, 0:n], source[:, bass.ds(c * CHUNK, n)], ACT.Relu,
                                           bias=bn_col[:, 0, 3:4], scale=bn_col[:, 0, 1:2]).then_inc(relued, 1)
                        act.wait_ge(made[layer], c + 1)
                        act.activation(out[:, bass.ds(c * CHUNK, n)], ps[:, s, 0:n], ACT.Identity,
                                       bias=colvec[:, bias:bias + 1]).then_inc(kept[layer], 1)
                    over_chunks(act, keep)

                @block.vector
                def _(dve, layer=layer, bias=bias, out=out):
                    def measure(c, s, n):
                        dve.wait_ge(kept[layer], c + 1)
                        dve.bn_stats(bn_parts[:, bass.ds(c, 1), :].rearrange("p o s -> p (o s)"),
                                     out[:, bass.ds(c * CHUNK, n)]).then_inc(stats[layer], 1)
                    over_chunks(dve, measure)
                    dve.wait_ge(stats[layer], CHUNKS + 1)
                    k = [0]

                    def link(ins):
                        k[0] += 1
                        ins.then_inc(ready[layer], 1)
                        dve.wait_ge(ready[layer], k[0])
                    link(dve.bn_aggr(bn_out[:, layer, :], bn_parts[:]))
                    dve.wait_ge(bn_root[layer], 2)
                    link(dve.tensor_tensor(bn_col[:, layer, 1:2], bn_col[:, layer, 0:1],
                                           colvec[:, bias + 1:bias + 2], ALU.mult))
                    link(dve.tensor_tensor(bn_col[:, layer, 2:3], bn_out[:, layer, 0:1],
                                           bn_col[:, layer, 1:2], ALU.mult))
                    link(dve.tensor_tensor(bn_col[:, layer, 3:4], colvec[:, bias + 2:bias + 3],
                                           bn_col[:, layer, 2:3], ALU.subtract))

        xr_in, out_done = [sem("xr_in0"), sem("xr_in1")], [sem("out0"), sem("out1")]
        relu2, turned2, summed, ln_step, normed = (sem(n) for n in ("relu2", "turned2", "summed", "ln_step", "normed"))
        ln_root = sem("ln_root")
        LN_LINKS = 2
        with nc.Block() as block:
            @block.gpsimd
            def _(pool):
                def root(c, s, n):
                    pool.wait_ge(ln_step, c * LN_LINKS + 2)
                    q = n // PER
                    inverse_root(pool, ln_rstd[0:q, s, :], ln_out[0:q, s, :, 1], eps[0:q, 0:PER], minus_half[0:q, 0:PER],
                                 ln_root, 2 * c + 1)
                over_chunks(pool, root)

            @block.sync
            def _(sp):
                def store(c, s, n):
                    sp.wait_ge(normed, c + 1)
                    sp.dma_start(rows_of(a["out"], c, n), stage_o[0:n // PER, s, :]).then_inc(out_done[s], 16)
                over_chunks(sp, store)
                sp.wait_ge(out_done[0], 16 * (CHUNKS // 2 + 1))
                sp.wait_ge(out_done[1], 16 * (CHUNKS // 2))

            @block.scalar
            def _(act):
                def relu(c, s, n):
                    wait(act, summed, c - 1)
                    act.dma_start(stage_x[0:n // PER, s, :], rows_of(a["x"], c, n)).then_inc(xr_in[s], 16)
                    wait(act, turned2, c - 1)
                    act.activation(stage_h[:, s, 0:n], y2[:, bass.ds(c * CHUNK, n)], ACT.Relu,
                                   bias=bn_col[:, 1, 3:4], scale=bn_col[:, 1, 1:2]).then_inc(relu2, 1)
                over_chunks(act, relu)

            @block.tensor
            def _(pe):
                def to_rows(c, s, n):
                    pe.wait_ge(relu2, c + 1)
                    wait(pe, summed, c - 1)
                    turn(pe, s, stage_h[:, s, :], n).then_inc(turned2, 1)
                over_chunks(pe, to_rows)

            @block.vector
            def _(dve):
                def normalize(c, s, n):
                    q = n // PER
                    dve.wait_ge(ln_root, 2 * c + 2)
                    for k in range(PER):
                        u = stage_o[0:q, s, k * D:(k + 1) * D]
                        ins = dve.tensor_scalar(u, u, ln_out[0:q, s, k, 0:1], ln_rstd[0:q, s, k:k + 1],
                                                ALU.subtract, ALU.mult)
                    ins.then_inc(normed, 1)

                def norm(c, s, n):
                    q = n // PER
                    dve.wait_ge(turned2, c + 1)
                    if isinstance(c, int):
                        dve.wait_ge(xr_in[s], 16 * (c // 2 + 1))
                        wait(dve, out_done[s], 16 * (c // 2))
                    else:
                        dve.wait_ge(xr_in[s], (c + (2 - s)) * 8)
                        dve.wait_ge(out_done[s], (c - s) * 8)
                    dve.tensor_tensor(stage_o[0:q, s, :], ps[0:q, s, :], stage_x[0:q, s, :], ALU.add
                                      ).then_inc(summed, 1)
                    dve.wait_ge(summed, c + 1)
                    for k in range(PER):
                        ins = dve.bn_stats(ln_parts[0:q, s, k, :], stage_o[0:q, s, k * D:(k + 1) * D])
                    ins.then_inc(ln_step, 1)
                    dve.wait_ge(ln_step, c * LN_LINKS + 1)
                    if not (isinstance(c, int) and c == 0):
                        normalize(c - 1, 1 - s, CHUNK)
                    for k in range(PER):
                        ins = dve.bn_aggr(ln_out[0:q, s, k, :], ln_parts[0:q, s, k, :])
                    ins.then_inc(ln_step, 1)
                over_chunks(dve, norm)
                normalize(CHUNKS, CHUNKS % 2, TAIL)


def kernel(x, src, dst, edge_attr_16, L0_gnn_ee_w1, L0_gnn_ee_b1, L0_gnn_ee_g1, L0_gnn_ee_bb1, L0_gnn_ee_w2,
           L0_gnn_ee_b2, L0_gnn_mlp_w1, L0_gnn_mlp_b1, L0_gnn_mlp_g1, L0_gnn_mlp_bb1, L0_gnn_mlp_w2,
           L0_gnn_mlp_b2, L0_gnn_mlp_g2, L0_gnn_mlp_bb2):
    import concourse.bacc as bacc
    from concourse.bass_utils import run_bass_kernel_spmd

    def laid(v):
        return np.ascontiguousarray(v)

    padded = TILES * P
    x, src, dst, edges = (np.asarray(v) for v in (x, src, dst, edge_attr_16))
    src_p = np.zeros(padded, src.dtype)
    src_p[:E] = src
    dst_p = np.full(padded, NO_NODE, dst.dtype)
    dst_p[:E] = dst
    edges_p = np.zeros((padded, ED), edges.dtype)
    edges_p[:E] = edges
    w1 = np.asarray(L0_gnn_ee_w1)
    w1bd = np.zeros((QUAD, ED, QUAD, D), w1.dtype)
    for q in range(QUAD):
        w1bd[q, :, q] = w1
    eye = np.eye(P, dtype=np.float32)
    arrays = {
        "x": laid(x), "x_t": laid(x.T),
        "src_tiles": laid(src_p.reshape(TILES, P).T), "dst_tiles": laid(dst_p.reshape(TILES, P).T),
        "dst_groups": laid(dst_p.reshape(GROUPS, GROUP_EDGES)),
        "edges": laid(edges_p.reshape(P, TILES * ED)),
        "edges_t": laid(edges_p.reshape(TILES // QUAD, QUAD, P, ED).transpose(1, 3, 0, 2)
                        .reshape(QUAD * ED, TILES // QUAD * P)),
        "ee_w1bd": laid(w1bd.reshape(QUAD * ED, QUAD * D)), "ee_w1": laid(w1), "ee_w2": laid(L0_gnn_ee_w2),
        "mlp_w1": laid(L0_gnn_mlp_w1), "mlp_w2": laid(L0_gnn_mlp_w2),
        "ee_b1": laid(L0_gnn_ee_b1), "ee_g1": laid(L0_gnn_ee_g1), "ee_bb1": laid(L0_gnn_ee_bb1),
        "ee_b2": laid(L0_gnn_ee_b2), "mlp_b1": laid(L0_gnn_mlp_b1), "mlp_g1": laid(L0_gnn_mlp_g1),
        "mlp_bb1": laid(L0_gnn_mlp_bb1), "mlp_b2": laid(L0_gnn_mlp_b2), "mlp_g2": laid(L0_gnn_mlp_g2),
        "mlp_bb2": laid(L0_gnn_mlp_bb2),
        "ident": eye, "iota": laid(np.tile(np.arange(WINDOW, dtype=np.float32), (P, 1))),
        "block_mask": laid(np.kron(np.eye(P // ED, dtype=np.float32), np.ones((ED, ED), np.float32))),
        "fold": laid(np.tile(np.eye(ED, dtype=np.float32), (P // ED, 1))),
    }
    nc = bacc.Bacc("TRN2", target_bir_lowering=False, num_devices=1)
    aps = {n: nc.dram_tensor(f"in_{n}", v.shape, mybir.dt.from_np(v.dtype), kind="ExternalInput").ap()
           for n, v in arrays.items()}
    aps["out"] = nc.dram_tensor("out_0", (N, D), F32, kind="ExternalOutput").ap()
    build(nc, aps)
    r = run_bass_kernel_spmd(nc, [{f"in_{n}": v for n, v in arrays.items()}], core_ids=[0])
    return r.results[0]["out_0"]
```

```python
from contextlib import ExitStack

import numpy as np
import concourse.bass as bass
from concourse import mybir

F32, F32R, I32, BF16 = mybir.dt.float32, mybir.dt.float32r, mybir.dt.int32, mybir.dt.bfloat16
ALU = mybir.AluOpType
ACT = mybir.ActivationFunctionType
AX_X = mybir.AxisListType.X

P = 128
N, E, D, ED = 12500, 212500, 128, 16
EPS = 1e-5
GROUP_TILES = 8
GROUP_EDGES = GROUP_TILES * P
GROUPS = -(-E // GROUP_EDGES)
TILES = GROUPS * GROUP_TILES
WINDOW = 96
ROUNDS_ALL = -(-N // WINDOW)
NT = ROUNDS_ALL * WINDOW + WINDOW
NO_NODE = 1 << 20
PAIR = 2
PARTS = 4
BODY = 4
BODIES = GROUPS // BODY
GROUP_COLS = GROUP_EDGES // PAIR
GRAM_COLS, GRAM_SLOTS = 1024, 4
GRAM_LOADS = TILES * ED // GRAM_COLS
GRAM_BODIES = GRAM_LOADS // GRAM_SLOTS
GRAM_REST = GRAM_LOADS % GRAM_SLOTS
CHUNK = 512
CHUNKS = N // CHUNK
TAIL = N - CHUNKS * CHUNK
PER = 4
BASE_ROWS = GROUPS // 2

assert GROUPS % BODY == 0 and TILES * ED % GRAM_COLS == 0 and CHUNKS % 4 == 0 and TAIL % PER == 0


def wait(engine, semaphore, value):
    if isinstance(value, int) and value <= 0:
        return
    engine.wait_ge(semaphore, value)


def inverse_root(pool, out, variance, eps, minus_half, semaphore, value):
    pool.tensor_tensor(out, variance, eps, ALU.add).then_inc(semaphore, 1)
    pool.wait_ge(semaphore, value)
    pool.tensor_tensor(out, out, minus_half, ALU.pow).then_inc(semaphore, 1)


def build(nc, a):
    with ExitStack() as ctx:
        def sb(name, shape, dt=F32):
            return ctx.enter_context(nc.sbuf_tensor(name, shape, dt))

        def sem(name):
            return ctx.enter_context(nc.semaphore(name))

        table = sb("table", [P, 2, NT])
        rows = sb("rows", [P, 4, GROUP_TILES * D])
        onehot = sb("onehot", [P, 2, GROUP_TILES, WINDOW])
        ea = sb("ea", [P, 2, 2 * GROUP_COLS])
        ea_high = sb("ea_high", [P, 2, GROUP_COLS], F32R)
        ea_parts = sb("ea_parts", [P, 2, GROUP_COLS], F32R)
        dst_i = sb("dst_i", [P, TILES], I32)
        dst_f = sb("dst_f", [P, TILES])
        rel = sb("rel", [P, TILES])
        idx = sb("idx", [P, 2, 2 * GROUP_TILES], I32)
        iota = sb("iota_sb", [P, WINDOW])
        ident = sb("ident_sb", [P, P])
        block_mask = sb("block_mask_sb", [P, P])
        fold = sb("fold_sb", [P, ED])
        ones = sb("ones", [P, P])
        minus_half = sb("minus_half", [P, D])
        eps = sb("eps", [P, D])
        ones_bf = sb("ones_bf", [P, P], BF16)
        ee_w1bd = sb("ee_w1bd_sb", [P, PAIR * D])
        ee_w1f = sb("ee_w1f", [P, PAIR * D])
        ee_w1high = sb("ee_w1high", [P, PAIR * D], F32R)
        ee_w1parts = sb("ee_w1parts", [P, PAIR * D], F32R)
        ee_shift = sb("ee_shift", [P, D])
        ee_negshift = sb("ee_negshift", [P, D])
        shift_col = sb("shift_col", [P, 1])
        per_edge = sb("per_edge", [P, 1])
        low_rows = sb("low_rows_sb", [P, 2])
        ee_w1 = sb("ee_w1_sb", [ED, D])
        ee_w2 = sb("ee_w2_sb", [D, D])
        mlp_w1 = sb("mlp_w1_sb", [D, D])
        mlp_w2 = sb("mlp_w2_sb", [D, D])
        rowvec = sb("rowvec", [P, 3, D])
        colvec = sb("colvec", [P, 7])
        stage_x = sb("stage_x", [P, 2, CHUNK])
        stage_h = sb("stage_h", [P, 2, CHUNK])
        stage_o = sb("stage_o", [P, 2, CHUNK])
        part = sb("part", [P, GRAM_LOADS, ED])
        part1 = sb("part1", [P, ED])
        gram = sb("gram", [P, P])
        gram1 = sb("gram1", [P, ED])
        mean_row = sb("mean_row", [1, ED])
        mean_col = sb("mean_col", [ED, 1])
        cov = sb("cov", [ED, ED])
        cov1 = sb("cov1", [ED, ED])
        prod = sb("prod", [ED, 2, D])
        bnrow = sb("bnrow", [P, 5, D])
        base_min = sb("base_min", [BASE_ROWS, 2])
        base0 = sb("base0", [P, GROUPS])
        base = sb("base", [P, GROUPS])
        base_i = sb("base_i", [1, GROUPS], I32)
        wide = sb("wide", [P, 4])
        rounds_i = sb("rounds_i", [1, 1], I32)
        bn_parts = sb("bn_parts", [P, CHUNKS + 1, 6])
        bn_out = sb("bn_out", [P, 2, 2])
        bn_col = sb("bn_col", [P, 2, 4])
        summed = sb("summed", [P, 2, CHUNK])
        ln_parts = sb("ln_parts", [P, 4, PER, 6])
        ln_out = sb("ln_out", [P, 4, PER, 2])
        ln_root = sb("ln_root", [P, 4, PER])
        ln_rstd = sb("ln_rstd", [P, 4, 2, PER])
        ps = ctx.enter_context(nc.psum_tensor("ps", [P, 8, 512], F32))

        base_dram = nc.dram_tensor("base_scratch", (GROUPS,), F32, kind="Internal").ap()
        h_dram = nc.dram_tensor("h_scratch", (N, D), F32, kind="Internal").ap()

        weights_in, dst_in, groups_in, base_out, base_in = (
            sem(n) for n in ("weights_in", "dst_in", "groups_in", "base_out", "base_in"))
        gram_in = [sem(f"gram_in{s}") for s in range(GRAM_SLOTS)]
        gram_summed, gram_done = sem("gram_summed"), sem("gram_done")
        base_ready, step, pe_step, cleared = sem("base_ready"), sem("step"), sem("pe_step"), sem("cleared")
        root_ready = sem("root_ready")
        WEIGHTS = 13 + 7

        with nc.Block() as block:
            @block.sync
            def _(sp):
                sp.dma_start(table[0:BASE_ROWS, 1, 0:2 * GROUP_EDGES].bitcast(I32),
                             a["dst_groups"].rearrange("(r two) e -> r (two e)", two=2)).then_inc(groups_in, 16)
                sp.dma_start(dst_i[:], a["dst_tiles"]).then_inc(dst_in, 16)

                def load(s, n):
                    sp.dma_start(rows[:, s, 0:GRAM_COLS],
                                 a["edges"][:, bass.ds(n * GRAM_COLS, GRAM_COLS)]).then_inc(gram_in[s], 16)
                def reload(s, i):
                    sp.wait_ge(gram_done, i * GRAM_SLOTS + (s + 1 - GRAM_SLOTS))
                    sp.wait_ge(gram_summed, i * GRAM_SLOTS + (s + 1 - GRAM_SLOTS))
                    load(s, i * GRAM_SLOTS + s)

                for s in range(GRAM_SLOTS):
                    load(s, s)
                with sp.Fori(1, GRAM_BODIES) as i:
                    for s in range(GRAM_SLOTS):
                        reload(s, i)
                for s in range(GRAM_REST):
                    reload(s, GRAM_BODIES)

            @block.scalar
            def _(act):
                for t, n in ((ident, "ident"), (iota, "iota"), (block_mask, "block_mask"), (fold, "fold"),
                             (ee_w1bd, "ee_w1bd"), (low_rows, "low_rows"), (ee_w1, "ee_w1"), (ee_w2, "ee_w2"),
                             (mlp_w1, "mlp_w1"), (mlp_w2, "mlp_w2")):
                    act.dma_start(t[:], a[n]).then_inc(weights_in, 16)
                for k, n in enumerate(("ee_b1", "ee_g1", "ee_bb1")):
                    act.dma_start(rowvec[:, k, :], a[n].rearrange("(o d) -> o d", o=1).broadcast_to([P, D])
                                  ).then_inc(weights_in, 16)
                for k, n in enumerate(("ee_b2", "mlp_b1", "mlp_g1", "mlp_bb1", "mlp_b2", "mlp_g2", "mlp_bb2")):
                    act.dma_start(colvec[:, k:k + 1], a[n].rearrange("(d o) -> d o", o=1)).then_inc(weights_in, 16)
                act.wait_ge(base_ready, 1)
                act.dma_start(base_dram.rearrange("(r two) -> r two", two=2), base_min[:]).then_inc(base_out, 16)
                act.wait_ge(base_out, 16)
                act.dma_start(base0[:], base_dram.rearrange("(o g) -> o g", o=1).broadcast_to([P, GROUPS])
                              ).then_inc(base_in, 16)

            @block.gpsimd
            def _(pool):
                pool.memset(ones[:], 1.0).then_inc(cleared, 1)
                pool.memset(ones_bf[:], 1.0).then_inc(cleared, 1)
                pool.memset(minus_half[:], -0.5).then_inc(cleared, 1)
                pool.memset(eps[:], EPS).then_inc(cleared, 1)
                pool.memset(table[:, 0, :], 0.0).then_inc(cleared, 1)
                pool.wait_ge(base_ready, 1)
                pool.memset(table[:, 1, :], 0.0).then_inc(cleared, 1)
                pool.wait_ge(step, 14)
                pool.wait_ge(cleared, 4)
                inverse_root(pool, bnrow[:, 0, :], bnrow[:, 2, :], eps[:], minus_half[:], root_ready, 1)

            @block.tensor
            def _(pe):
                def gram_slot(n, s, i):
                    pe.wait_ge(gram_in[s], 16 * (i + 1))
                    for b in range(GRAM_COLS // P):
                        x = rows[:, s, b * P:(b + 1) * P]
                        mm = pe.matmul(ps[:, 0, 0:P], x, x, start=(n == 0 and b == 0), stop=True,
                                       skip_group_check=True)
                    mm.then_inc(gram_done, 1)
                for s in range(GRAM_SLOTS):
                    gram_slot(s, s, 0)
                with pe.Fori(1, GRAM_BODIES) as i:
                    for s in range(GRAM_SLOTS):
                        gram_slot(None, s, i)
                for s in range(GRAM_REST):
                    gram_slot(None, s, GRAM_BODIES)
                pe.wait_ge(cleared, 1)
                pe.wait_ge(step, 6)
                pe.wait_ge(weights_in, 16 * WEIGHTS)
                pe.matmul(ps[0:1, 1, 0:ED], ones[:, 0:1], part1[:], start=True, stop=True)
                pe.matmul(ps[0:ED, 2, 0:1], part1[:], ones[:, 0:1], start=True, stop=True)
                pe.matmul(ps[:, 2, 8:9], ones[:], wide[:, 0:1], start=True, stop=True)
                pe.matmul(ps[:, 3, 0:ED], gram[:], fold[:], start=True, stop=True).then_inc(pe_step, 1)
                pe.wait_ge(step, 9)
                pe.matmul(ps[0:ED, 4, 0:ED], fold[:], gram1[:], start=True, stop=True)
                pe.matmul(ps[0:ED, 5, 0:ED], mean_row[:], mean_row[:], start=True, stop=True).then_inc(pe_step, 1)
                pe.wait_ge(step, 11)
                pe.matmul(ps[0:ED, 6, 0:D], cov[:], ee_w1[:], start=True, stop=True).then_inc(pe_step, 1)
                pe.wait_ge(step, 13)
                pe.matmul(ps[:, 7, 0:D], ones[0:ED, :], prod[:, 0, :], start=True, stop=True)
                pe.matmul(ps[:, 7, D:2 * D], ones[0:ED, :], prod[:, 1, :], start=True, stop=True
                          ).then_inc(pe_step, 1)
                pe.wait_ge(step, 19)
                pe.matmul(ps[:, 0, 0:1], ee_shift[0:1, :], ones[0:1, 0:1], start=True, stop=True).then_inc(pe_step, 1)
                pe.wait_ge(step, 22)
                pe.matmul(ps[:, 1, 0:1], ee_w2[:], shift_col[:], start=True, stop=True).then_inc(pe_step, 1)

            @block.vector
            def _(dve):
                steps = [0]

                def link(ins):
                    steps[0] += 1
                    ins.then_inc(step, 1)
                    dve.wait_ge(step, steps[0])

                dve.wait_ge(groups_in, 16)
                dve.tensor_reduce(base_min[:], table[0:BASE_ROWS, 1, 0:2 * GROUP_EDGES].bitcast(I32)
                                  .rearrange("r (two e) -> r two e", two=2), AX_X, ALU.min).then_inc(base_ready, 1)
                dve.wait_ge(dst_in, 16)
                dve.tensor_copy(dst_f[:], dst_i[:]).then_inc(base_ready, 1)

                dve.wait_ge(base_in, 16)
                dve.wait_ge(base_ready, 2)
                link(dve.tensor_tensor(rel[:].rearrange("p (g t) -> p g t", t=GROUP_TILES),
                                       dst_f[:].rearrange("p (g t) -> p g t", t=GROUP_TILES),
                                       base0[:].unsqueeze(2).broadcast_to([P, GROUPS, GROUP_TILES]), ALU.subtract))
                link(dve.tensor_scalar(dst_i[:].bitcast(F32), rel[:], NO_NODE / 2.0, None, ALU.is_lt))
                link(dve.scalar_tensor_tensor(rel[:], rel[:], float(WINDOW), dst_i[:].bitcast(F32),
                                              ALU.is_ge, ALU.mult))
                link(dve.tensor_reduce(wide[:, 0:1], rel[:], AX_X, ALU.max))

                def sum_slot(s, i):
                    dve.wait_ge(gram_in[s], 16 * (i + 1))
                    dve.tensor_reduce(part[:, bass.ds(i * GRAM_SLOTS + s, 1), :],
                                      rows[:, s, 0:GRAM_COLS].rearrange("p (n c) -> p c n", c=ED),
                                      AX_X, ALU.add).then_inc(gram_summed, 1)
                with dve.Fori(0, GRAM_BODIES) as i:
                    for s in range(GRAM_SLOTS):
                        sum_slot(s, i)
                for s in range(GRAM_REST):
                    sum_slot(s, GRAM_BODIES)
                dve.wait_ge(gram_summed, GRAM_LOADS)
                link(dve.tensor_reduce(part1[:], part[:].rearrange("p n c -> p c n"), AX_X, ALU.add))
                dve.wait_ge(gram_done, GRAM_LOADS)
                dve.wait_ge(weights_in, 16 * WEIGHTS)
                link(dve.tensor_tensor(gram[:], ps[:, 0, 0:P], block_mask[:], ALU.mult))
                dve.wait_ge(pe_step, 1)
                link(dve.tensor_scalar(mean_row[:], ps[0:1, 1, 0:ED], 1.0 / E, None, ALU.mult))
                link(dve.tensor_scalar(mean_col[:], ps[0:ED, 2, 0:1], 1.0 / E, None, ALU.mult))
                link(dve.tensor_copy(gram1[:], ps[:, 3, 0:ED]))
                dve.wait_ge(pe_step, 2)
                link(dve.tensor_scalar(cov1[:], ps[0:ED, 4, 0:ED], 1.0 / E, None, ALU.mult))
                link(dve.tensor_tensor(cov[:], cov1[:], ps[0:ED, 5, 0:ED], ALU.subtract))
                dve.wait_ge(pe_step, 3)
                link(dve.tensor_tensor(prod[:, 0, :], ps[0:ED, 6, 0:D], ee_w1[:], ALU.mult))
                link(dve.tensor_scalar(prod[:, 1, :], ee_w1[:], mean_col[:, 0:1], None, ALU.mult))
                dve.wait_ge(pe_step, 4)
                link(dve.tensor_copy(bnrow[:, 2, :], ps[:, 7, 0:D]))
                dve.wait_ge(root_ready, 2)
                link(dve.tensor_tensor(bnrow[:, 1, :], bnrow[:, 0, :], rowvec[:, 1, :], ALU.mult))
                link(dve.tensor_tensor(bnrow[:, 2, :], ps[:, 7, D:2 * D], rowvec[:, 0, :], ALU.add))
                link(dve.tensor_tensor(bnrow[:, 3, :], rowvec[:, 0, :], bnrow[:, 2, :], ALU.subtract))
                link(dve.tensor_tensor(bnrow[:, 4, :], bnrow[:, 3, :], bnrow[:, 1, :], ALU.mult))
                link(dve.tensor_tensor(ee_shift[:], bnrow[:, 4, :], rowvec[:, 2, :], ALU.add))
                dve.tensor_scalar(ee_negshift[:], ee_shift[:], -1.0, None, ALU.mult)
                link(dve.tensor_tensor(ee_w1f[:].rearrange("r (q d) -> r q d", q=PAIR),
                                       ee_w1bd[:].rearrange("r (q d) -> r q d", q=PAIR),
                                       bnrow[:, 1:2, :].broadcast_to([P, PAIR, D]), ALU.mult))
                link(dve.tensor_scalar(ee_w1high[:], ee_w1f[:], low_rows[:, 1:2], None, ALU.mult))
                dve.tensor_tensor(ee_w1parts[:], ee_w1f[:], ee_w1high[:].bitcast(F32), ALU.subtract)
                dve.wait_ge(pe_step, 5)
                link(dve.tensor_copy(shift_col[:], ps[:, 0, 0:1]))
                dve.wait_ge(pe_step, 6)
                link(dve.tensor_tensor(per_edge[:], ps[:, 1, 0:1], colvec[:, 0:1], ALU.add))
                link(dve.tensor_scalar(wide[:, 1:2], ps[:, 2, 8:9], 0.5, None, ALU.is_ge))
                link(dve.tensor_scalar(wide[:, 2:3], wide[:, 1:2], -1.0, 1.0, ALU.mult, ALU.add))
                link(dve.tensor_scalar(rounds_i[:], wide[0:1, 1:2], float(ROUNDS_ALL - 1), 1.0, ALU.mult, ALU.add))

        ea_in = [sem("ea_in0"), sem("ea_in1")]
        high_done, parts_done, features_done, clamped, onehot_done, sums_done, added = (
            sem(n) for n in ("high_done", "parts_done", "features_done", "clamped", "onehot_done", "sums_done", "added"))
        idx_in = [sem("idx_in0"), sem("idx_in1")]
        gathering = sem("gathering")
        gathered = [sem(f"gathered{s}") for s in range(4)]
        round_sems = [*ea_in, high_done, parts_done, features_done, clamped, onehot_done, sums_done, added, *idx_in, gathering, *gathered]

        def rewind():
            with nc.Block() as block:
                @block.vector
                def _(dve):
                    dve.tensor_scalar(base[:], base0[:], wide[:, 2:3], None, ALU.mult)

        def open_round():
            with nc.Block() as block:
                @block.gpsimd
                def _(pool):
                    for s in round_sems:
                        pool.sem_clear(s)

                @block.vector
                def _(dve):
                    dve.tensor_tensor(rel[:].rearrange("p (g t) -> p g t", t=GROUP_TILES),
                                      dst_f[:].rearrange("p (g t) -> p g t", t=GROUP_TILES),
                                      base[:].unsqueeze(2).broadcast_to([P, GROUPS, GROUP_TILES]), ALU.subtract)
                    dve.tensor_copy(base_i[:], base[0:1, :])

        def window_sums(dve, kinds):
            def make_onehot(g, u):
                wait(dve, sums_done, g - 1)
                dve.tensor_tensor(onehot[:, u % 2],
                                  iota[:].unsqueeze(1).broadcast_to([P, GROUP_TILES, WINDOW]),
                                  rel[:, bass.ds(g * GROUP_TILES, GROUP_TILES)].unsqueeze(2)
                                  .broadcast_to([P, GROUP_TILES, WINDOW]), ALU.is_equal).then_inc(onehot_done, 1)

            def clamp(g, u):
                dve.wait_ge(features_done, g + 1)
                wait(dve, sums_done, g - 1)
                b = 2 * (u % 2)
                dve.tensor_tensor(rows[:, u % 2, :].rearrange("p (t d) -> p t d", d=D),
                                  ps[:, b:b + 2, :].rearrange("p b (t d) -> p (b t) d", d=D),
                                  ee_negshift[:].unsqueeze(1).broadcast_to([P, GROUP_TILES, D]), ALU.max
                                  ).then_inc(clamped, 1)

            def add_window(g, u):
                at = dve.value_load(base_i[0:1, bass.ds(g, 1)], min_val=0, max_val=NT - WINDOW)
                dve.wait_ge(sums_done, g + 1)
                wait(dve, added, g)
                here = table[:, 0:kinds, bass.ds(at, WINDOW)]
                dve.tensor_tensor(here, here, ps[:, 4 + 2 * (u % 2):4 + 2 * (u % 2) + kinds, 0:WINDOW], ALU.add
                                  ).then_inc(added, 1)

            def body(i, last=False):
                for u in range(BODY):
                    if not (last and u == BODY - 1):
                        make_onehot(i * BODY + u + 1, u + 1)
                        if kinds == 2:
                            clamp(i * BODY + u + 1, u + 1)
                    add_window(i * BODY + u, u)

            make_onehot(0, 0)
            if kinds == 2:
                clamp(0, 0)
            body(0)
            with dve.Fori(1, BODIES - 1) as i:
                body(i)
            body(BODIES - 1, last=True)
            dve.tensor_scalar(base[:], base[:], float(WINDOW), None, ALU.add)

        rewind()
        nc.all_engine_barrier()
        rounds = nc.values_load(rounds_i[0:1, 0:1], min_val=1, max_val=ROUNDS_ALL)
        with nc.Fori(0, rounds):
            open_round()
            with nc.Block() as block:
                @block.sync
                def _(sp):
                    def load(i, s):
                        for part in range(PARTS):
                            sp.dma_start(ea[part * PAIR * ED:(part + 1) * PAIR * ED, s, :],
                                         a["edges_t"][:, bass.ds((i * 2 + s) * 2 * GROUP_COLS, 2 * GROUP_COLS)]
                                         ).then_inc(ea_in[s], 16)
                    load(0, 0)
                    load(0, 1)
                    with sp.Fori(1, BODIES) as i:
                        for s in range(2):
                            sp.wait_ge(parts_done, i * BODY + (2 * s - 2))
                            load(i, s)

                @block.scalar
                def _(act):
                    def high(i, u):
                        if u % 2 == 0:
                            act.wait_ge(ea_in[u // 2], 16 * PARTS * (i + 1))
                        wait(act, parts_done, i * BODY + (u - 1))
                        act.activation(ea_high[:, u % 2, :], ea[:, u // 2, (u % 2) * GROUP_COLS:(u % 2 + 1) * GROUP_COLS],
                                       ACT.Copy, scale=low_rows[:, 0:1]).then_inc(high_done, 1)
                    for u in range(BODY):
                        high(0, u)
                    with act.Fori(1, BODIES) as i:
                        for u in range(BODY):
                            high(i, u)

                @block.gpsimd
                def _(pool):
                    def split(i, u):
                        wait(pool, features_done, i * BODY + (u - 1))
                        pool.wait_ge(high_done, i * BODY + u + 1)
                        pool.tensor_tensor(ea_parts[:, u % 2, :],
                                           ea[:, u // 2, (u % 2) * GROUP_COLS:(u % 2 + 1) * GROUP_COLS],
                                           ea_high[:, u % 2, :].bitcast(F32), ALU.subtract).then_inc(parts_done, 1)
                    for u in range(BODY):
                        split(0, u)
                    with pool.Fori(1, BODIES) as i:
                        for u in range(BODY):
                            split(i, u)

                @block.tensor
                def _(pe):
                    def features(g, u):
                        wait(pe, clamped, g - 1)
                        pe.wait_ge(parts_done, g + 1)
                        for pair in range(GROUP_TILES // PAIR):
                            mm = pe.matmul(ps[:, 2 * (u % 2) + pair // 2, (pair % 2) * PAIR * D:(pair % 2 + 1) * PAIR * D],
                                           ea_parts[:, u % 2, pair * P:(pair + 1) * P], ee_w1parts[:],
                                           start=True, stop=True)
                        mm.then_inc(features_done, 1)

                    def sums(g, u):
                        wait(pe, added, g - 1)
                        pe.wait_ge(onehot_done, g + 1)
                        for t in range(GROUP_TILES):
                            pe.matmul(ps[:, 5 + 2 * (u % 2), 0:WINDOW], ones_bf[:],
                                      onehot[:, u % 2, t, :].bitcast(BF16)[:, 1:2 * WINDOW:2],
                                      start=(t == 0), stop=(t == GROUP_TILES - 1))
                        pe.wait_ge(clamped, g + 1)
                        for t in range(GROUP_TILES):
                            mm = pe.matmul(ps[:, 4 + 2 * (u % 2), 0:WINDOW], rows[:, u % 2, t * D:(t + 1) * D],
                                           onehot[:, u % 2, t, :], start=(t == 0), stop=(t == GROUP_TILES - 1))
                        mm.then_inc(sums_done, 1)

                    def body(i, last=False):
                        for u in range(BODY):
                            g = i * BODY + u
                            if not (last and u == BODY - 1):
                                features(g + 1, u + 1)
                            sums(g, u)

                    features(0, 0)
                    body(0)
                    with pe.Fori(1, BODIES - 1) as i:
                        body(i)
                    body(BODIES - 1, last=True)

                @block.vector
                def _(dve):
                    window_sums(dve, kinds=2)

        x_in, h_out = [sem("x_in0"), sem("x_in1")], [sem("h_out0"), sem("h_out1")]
        projected, h_half, h_ready, h_kept, turned, h_copied = (
            sem(n) for n in ("projected", "h_half", "h_ready", "h_kept", "turned", "h_copied"))

        def over_chunks(engine, step_of, slots=2):
            for s in range(slots):
                step_of(s, s, CHUNK)
            with engine.Fori(1, CHUNKS // slots) as i:
                for s in range(slots):
                    step_of(i * slots + s, s, CHUNK)
            step_of(CHUNKS, CHUNKS % slots, TAIL)

        def uses(c, s):
            return (c // 2) * 16 if isinstance(c, int) else (c - s) * 8

        def turn(pe, bank, source, n):
            for k in range(PER):
                tr = pe.transpose(ps[0:n // PER, bank, k * D:(k + 1) * D], source[:, k:n:PER], ident[:])
            return tr

        def rows_of(dram, c, n):
            return dram[bass.ds(c * CHUNK, n), :].rearrange("(p k) d -> p (k d)", k=PER)

        with nc.Block() as block:
            @block.sync
            def _(sp):
                def load(c, s, n):
                    wait(sp, h_ready, c - 1)
                    sp.dma_start(stage_x[:, s, 0:n], a["x_t"][:, bass.ds(c * CHUNK, n)]).then_inc(x_in[s], 16)
                over_chunks(sp, load)

            @block.gpsimd
            def _(pool):
                def store(c, s, n):
                    pool.wait_ge(h_copied, c + 1)
                    pool.dma_start(rows_of(h_dram, c, n), stage_o[0:n // PER, s, :]).then_inc(h_out[s], 16)
                over_chunks(pool, store)
                pool.wait_ge(h_out[0], 16 * (CHUNKS // 2 + 1))
                pool.wait_ge(h_out[1], 16 * (CHUNKS // 2))

            @block.tensor
            def _(pe):
                def project(c, s, n):
                    wait(pe, h_half, c - 1)
                    pe.matmul(ps[:, s, 0:n], ee_w2[:], table[:, 0, bass.ds(c * CHUNK, n)], start=True, stop=True
                              ).then_inc(projected, 1)
                    if not (isinstance(c, int) and c == 0):
                        turn_h(c - 1, 1 - s, CHUNK)

                def turn_h(c, s, n):
                    pe.wait_ge(h_ready, c + 1)
                    wait(pe, h_copied, c - 1)
                    turn(pe, 2 + s, stage_h[:, s, :], n).then_inc(turned, 1)
                over_chunks(pe, project)
                turn_h(CHUNKS, 0, TAIL)

            @block.vector
            def _(dve):
                def combine(c, s, n):
                    dve.wait_ge(projected, c + 1)
                    wait(dve, turned, c - 1)
                    wait(dve, h_kept, c - 1)
                    dve.scalar_tensor_tensor(stage_h[:, s, 0:n], table[:, 1, bass.ds(c * CHUNK, n)], per_edge[:, 0:1],
                                             ps[:, s, 0:n], ALU.mult, ALU.add).then_inc(h_half, 1)
                    dve.wait_ge(x_in[s], uses(c, s) + 16)
                    dve.wait_ge(h_half, c + 1)
                    dve.tensor_tensor(stage_h[:, s, 0:n], stage_h[:, s, 0:n], stage_x[:, s, 0:n], ALU.add
                                      ).then_inc(h_ready, 1)
                over_chunks(dve, combine)

            @block.scalar
            def _(act):
                def keep(c, s, n):
                    act.wait_ge(h_ready, c + 1)
                    act.copy(table[:, 0, bass.ds(c * CHUNK, n)], stage_h[:, s, 0:n]).then_inc(h_kept, 1)
                    act.wait_ge(turned, c + 1)
                    wait(act, h_out[s], uses(c, s))
                    act.copy(stage_o[0:n // PER, s, :], ps[0:n // PER, 2 + s, :]).then_inc(h_copied, 1)
                over_chunks(act, keep)

        rewind()
        with nc.Fori(0, rounds):
            open_round()
            with nc.Block() as block:
                @block.sync
                def _(sp):
                    def load(i, s):
                        sp.dma_start(idx[:, s, :], a["src_tiles"][:, bass.ds((i * 2 + s) * 2 * GROUP_TILES,
                                                                             2 * GROUP_TILES)]).then_inc(idx_in[s], 16)
                    load(0, 0)
                    load(0, 1)
                    with sp.Fori(1, BODIES) as i:
                        for s in range(2):
                            sp.wait_ge(gathered[2 * s], i * (16 * GROUP_TILES))
                            sp.wait_ge(gathered[2 * s + 1], i * (16 * GROUP_TILES))
                            load(i, s)

                @block.gpsimd
                def _(pool):
                    def body(i):
                        for u in range(BODY):
                            if u % 2 == 0:
                                pool.wait_ge(idx_in[u // 2], 16 * (i + 1))
                            wait(pool, sums_done, i * BODY + (u - 3))
                            pool.sem_inc(gathering, 1)
                            for t in range(GROUP_TILES):
                                k = (u % 2) * GROUP_TILES + t
                                pool.indirect_dma_start(
                                    rows[:, u, t * D:(t + 1) * D], None, h_dram,
                                    bass.IndirectOffsetOnAxis(ap=idx[:, u // 2, k:k + 1], axis=0)
                                ).then_inc(gathered[u], 16)
                    body(0)
                    with pool.Fori(1, BODIES) as i:
                        body(i)

                @block.tensor
                def _(pe):
                    def body(i):
                        for u in range(BODY):
                            g = i * BODY + u
                            wait(pe, added, g - 1)
                            pe.wait_ge(onehot_done, g + 1)
                            pe.wait_ge(gathered[u], (i + 1) * (16 * GROUP_TILES))
                            for t in range(GROUP_TILES):
                                mm = pe.matmul(ps[:, 4 + 2 * (u % 2), 0:WINDOW], rows[:, u, t * D:(t + 1) * D],
                                               onehot[:, u % 2, t, :], start=(t == 0), stop=(t == GROUP_TILES - 1))
                            mm.then_inc(sums_done, 1)
                    body(0)
                    with pe.Fori(1, BODIES) as i:
                        body(i)

                @block.vector
                def _(dve):
                    window_sums(dve, kinds=1)

        made, kept, stats, ready, bn_root = ([sem(f"{n}{k}") for k in range(2)]
                                    for n in ("made", "kept", "stats", "bn_ready", "bn_root"))
        relued = sem("relued")
        z, y1, y2 = table[:, 0], table[:, 1], table[:, 0]
        for layer in range(2):
            weight, bias = (mlp_w1, 1) if layer == 0 else (mlp_w2, 4)
            source, out = (z, y1) if layer == 0 else (y1, y2)
            with nc.Block() as block:
                @block.gpsimd
                def _(pool, layer=layer):
                    pool.wait_ge(ready[layer], 1)
                    inverse_root(pool, bn_col[:, layer, 0:1], bn_out[:, layer, 1:2], eps[:, 0:1], minus_half[:, 0:1],
                                 bn_root[layer], 1)

                @block.tensor
                def _(pe, layer=layer, weight=weight, source=source):
                    def dense(c, s, n):
                        wait(pe, kept[layer], c - 3)
                        if layer:
                            pe.wait_ge(relued, c + 1)
                        moving = stage_h[:, s % 2, 0:n] if layer else source[:, bass.ds(c * CHUNK, n)]
                        pe.matmul(ps[:, s, 0:n], weight[:], moving, start=True, stop=True).then_inc(made[layer], 1)
                    over_chunks(pe, dense, slots=4)

                @block.scalar
                def _(act, layer=layer, bias=bias, source=source, out=out):
                    def relu(c, s, n):
                        wait(act, made[1], c - 1)
                        act.activation(stage_h[:, s % 2, 0:n], source[:, bass.ds(c * CHUNK, n)], ACT.Relu,
                                       bias=bn_col[:, 0, 3:4], scale=bn_col[:, 0, 1:2]).then_inc(relued, 1)

                    def keep(c, s, n):
                        act.wait_ge(made[layer], c + 1)
                        act.activation(out[:, bass.ds(c * CHUNK, n)], ps[:, s, 0:n], ACT.Identity,
                                       bias=colvec[:, bias:bias + 1]).then_inc(kept[layer], 1)

                    def relu_and_keep(c, s, n):
                        relu(c, s, n)
                        if not (isinstance(c, int) and c == 0):
                            keep(c - 1, (s - 1) % 4, CHUNK)
                    if layer:
                        over_chunks(act, relu_and_keep, slots=4)
                        keep(CHUNKS, CHUNKS % 4, TAIL)
                    else:
                        over_chunks(act, keep, slots=4)

                @block.vector
                def _(dve, layer=layer, bias=bias, out=out):
                    def measure(c, s, n):
                        dve.wait_ge(kept[layer], c + 1)
                        dve.bn_stats(bn_parts[:, bass.ds(c, 1), :].rearrange("p o s -> p (o s)"),
                                     out[:, bass.ds(c * CHUNK, n)]).then_inc(stats[layer], 1)
                    over_chunks(dve, measure)
                    dve.wait_ge(stats[layer], CHUNKS + 1)
                    k = [0]

                    def link(ins):
                        k[0] += 1
                        ins.then_inc(ready[layer], 1)
                        dve.wait_ge(ready[layer], k[0])
                    link(dve.bn_aggr(bn_out[:, layer, :], bn_parts[:]))
                    dve.wait_ge(bn_root[layer], 2)
                    link(dve.tensor_tensor(bn_col[:, layer, 1:2], bn_col[:, layer, 0:1],
                                           colvec[:, bias + 1:bias + 2], ALU.mult))
                    link(dve.tensor_tensor(bn_col[:, layer, 2:3], bn_out[:, layer, 0:1],
                                           bn_col[:, layer, 1:2], ALU.mult))
                    link(dve.tensor_tensor(bn_col[:, layer, 3:4], colvec[:, bias + 2:bias + 3],
                                           bn_col[:, layer, 2:3], ALU.subtract))

        xr_in, out_done = [sem("xr_in0"), sem("xr_in1")], [sem("out0"), sem("out1")]
        relu2, residual, turned2, ln_stat, measured, rooted, ln_ready, normed = (
            sem(n) for n in ("relu2", "residual", "turned2", "ln_stat", "measured", "rooted", "ln_ready", "normed"))
        ln_inverse = sem("ln_inverse")
        SLOTS = 4

        def between(c, s, n):
            pass

        def lagging(engine, stages):
            def step_of(c, s, n):
                for k, stage in enumerate(stages):
                    if isinstance(c, int) and c < k:
                        break
                    stage(c - k, (s - k) % SLOTS, n if k == 0 else CHUNK)
            over_chunks(engine, step_of, slots=SLOTS)
            for late in range(1, len(stages)):
                for k in range(late, len(stages)):
                    c = CHUNKS + late - k
                    stages[k](c, c % SLOTS, TAIL if c == CHUNKS else CHUNK)

        with nc.Block() as block:
            @block.sync
            def _(sp):
                def load(c, s, n):
                    wait(sp, residual, c - 1)
                    sp.dma_start(stage_x[:, s % 2, 0:n], a["x_t"][:, bass.ds(c * CHUNK, n)]).then_inc(xr_in[s % 2], 16)

                def store(c, s, n):
                    sp.wait_ge(normed, c + 1)
                    sp.dma_start(rows_of(a["out"], c, n), stage_o[0:n // PER, s % 2, :]).then_inc(out_done[s % 2], 16)
                lagging(sp, [load, between, between, between, store])
                sp.wait_ge(out_done[0], 16 * (CHUNKS // 2 + 1))
                sp.wait_ge(out_done[1], 16 * (CHUNKS // 2))

            @block.gpsimd
            def _(pool):
                def add_x(c, s, n):
                    pool.wait_ge(relu2, c + 1)
                    pool.wait_ge(xr_in[s % 2], uses(c, s % 2) + 16)
                    wait(pool, turned2, c - 1)
                    pool.tensor_tensor(summed[:, s % 2, 0:n], stage_h[:, s % 2, 0:n], stage_x[:, s % 2, 0:n], ALU.add
                                       ).then_inc(residual, 1)
                over_chunks(pool, add_x, slots=SLOTS)

            @block.tensor
            def _(pe):
                def to_rows(c, s, n):
                    pe.wait_ge(residual, c + 1)
                    wait(pe, normed, c - 3)
                    turn(pe, s, summed[:, s % 2, :], n).then_inc(turned2, 1)
                over_chunks(pe, to_rows, slots=SLOTS)

            @block.vector
            def _(dve):
                def measure(c, s, n):
                    q = n // PER
                    dve.wait_ge(turned2, c + 1)
                    for k in range(PER):
                        ins = dve.bn_stats(ln_parts[0:q, s, k, :], ps[0:q, s, k * D:(k + 1) * D])
                    ins.then_inc(ln_stat, 1)

                def invert(c, s, n):
                    q = n // PER
                    dve.wait_ge(rooted, c + 1)
                    dve.reciprocal(ln_rstd[0:q, s, 0, :], ln_root[0:q, s, :]).then_inc(ln_inverse, 1)

                def aggregate(c, s, n):
                    q = n // PER
                    dve.wait_ge(ln_stat, c + 1)
                    if not isinstance(c, int) or c >= 2:
                        invert(c - 2, (s - 2) % SLOTS, CHUNK)
                    for k in range(PER):
                        ins = dve.bn_aggr(ln_out[0:q, s, k, :], ln_parts[0:q, s, k, :])
                    ins.then_inc(measured, 1)

                def shift(c, s, n):
                    q = n // PER
                    dve.wait_ge(ln_inverse, c + 1)
                    dve.scalar_tensor_tensor(ln_rstd[0:q, s, 1, :], ln_out[0:q, s, :, 0], -1.0, ln_rstd[0:q, s, 0, :],
                                             ALU.mult, ALU.mult).then_inc(ln_ready, 1)

                def step_of(c, s, n):
                    measure(c, s, n)
                    aggregate(c, s, n)
                    if not isinstance(c, int) or c >= 2:
                        shift(c - 2, (s - 2) % SLOTS, CHUNK)
                over_chunks(dve, step_of, slots=SLOTS)
                for c in (CHUNKS - 1, CHUNKS):
                    n = TAIL if c == CHUNKS else CHUNK
                    invert(c, c % SLOTS, n)
                    shift(c, c % SLOTS, n)

            @block.scalar
            def _(act):
                def relu(c, s, n):
                    wait(act, residual, c - 1)
                    act.activation(stage_h[:, s % 2, 0:n], y2[:, bass.ds(c * CHUNK, n)], ACT.Relu,
                                   bias=bn_col[:, 1, 3:4], scale=bn_col[:, 1, 1:2]).then_inc(relu2, 1)

                def root(c, s, n):
                    q = n // PER
                    act.wait_ge(measured, c + 1)
                    act.activation(ln_root[0:q, s, :], ln_out[0:q, s, :, 1], ACT.Sqrt, bias=eps[0:q, 0:1]
                                   ).then_inc(rooted, 1)

                def normalize(c, s, n):
                    q = n // PER
                    act.wait_ge(ln_ready, c + 1)
                    wait(act, out_done[s % 2], uses(c, s % 2))
                    for k in range(PER):
                        ins = act.activation(stage_o[0:q, s % 2, k * D:(k + 1) * D], ps[0:q, s, k * D:(k + 1) * D],
                                             ACT.Identity, bias=ln_rstd[0:q, s, 1, k:k + 1],
                                             scale=ln_rstd[0:q, s, 0, k:k + 1])
                    ins.then_inc(normed, 1)
                lagging(act, [relu, between, root, normalize])


def kernel(x, src, dst, edge_attr_16, L0_gnn_ee_w1, L0_gnn_ee_b1, L0_gnn_ee_g1, L0_gnn_ee_bb1, L0_gnn_ee_w2,
           L0_gnn_ee_b2, L0_gnn_mlp_w1, L0_gnn_mlp_b1, L0_gnn_mlp_g1, L0_gnn_mlp_bb1, L0_gnn_mlp_w2,
           L0_gnn_mlp_b2, L0_gnn_mlp_g2, L0_gnn_mlp_bb2):
    import concourse.bacc as bacc
    from concourse.bass_utils import run_bass_kernel_spmd

    def laid(v):
        return np.ascontiguousarray(v)

    padded = TILES * P
    x, src, dst, edges = (np.asarray(v) for v in (x, src, dst, edge_attr_16))
    src_p = np.zeros(padded, src.dtype)
    src_p[:E] = src
    dst_p = np.full(padded, NO_NODE, dst.dtype)
    dst_p[:E] = dst
    edges_p = np.zeros((padded, ED), edges.dtype)
    edges_p[:E] = edges
    w1 = np.asarray(L0_gnn_ee_w1)
    w1bd = np.zeros((PARTS, PAIR, ED, PAIR, D), w1.dtype)
    for q in range(PAIR):
        w1bd[:, q, :, q] = w1
    low = np.zeros((PARTS, PAIR * ED, 2), np.float32)
    low[1::2, :, 0] = 1.0
    low[2:, :, 1] = 1.0
    eye = np.eye(P, dtype=np.float32)
    arrays = {
        "x": laid(x), "x_t": laid(x.T),
        "src_tiles": laid(src_p.reshape(TILES, P).T), "dst_tiles": laid(dst_p.reshape(TILES, P).T),
        "dst_groups": laid(dst_p.reshape(GROUPS, GROUP_EDGES)),
        "edges": laid(edges_p.reshape(P, TILES * ED)),
        "edges_t": laid(edges_p.reshape(TILES // PAIR, PAIR, P, ED).transpose(1, 3, 0, 2)
                        .reshape(PAIR * ED, TILES // PAIR * P)),
        "ee_w1bd": laid(w1bd.reshape(P, PAIR * D)), "low_rows": laid(low.reshape(P, 2)), "ee_w1": laid(w1), "ee_w2": laid(L0_gnn_ee_w2),
        "mlp_w1": laid(L0_gnn_mlp_w1), "mlp_w2": laid(L0_gnn_mlp_w2),
        "ee_b1": laid(L0_gnn_ee_b1), "ee_g1": laid(L0_gnn_ee_g1), "ee_bb1": laid(L0_gnn_ee_bb1),
        "ee_b2": laid(L0_gnn_ee_b2), "mlp_b1": laid(L0_gnn_mlp_b1), "mlp_g1": laid(L0_gnn_mlp_g1),
        "mlp_bb1": laid(L0_gnn_mlp_bb1), "mlp_b2": laid(L0_gnn_mlp_b2), "mlp_g2": laid(L0_gnn_mlp_g2),
        "mlp_bb2": laid(L0_gnn_mlp_bb2),
        "ident": eye, "iota": laid(np.tile(np.arange(WINDOW, dtype=np.float32), (P, 1))),
        "block_mask": laid(np.kron(np.eye(P // ED, dtype=np.float32), np.ones((ED, ED), np.float32))),
        "fold": laid(np.tile(np.eye(ED, dtype=np.float32), (P // ED, 1))),
    }
    nc = bacc.Bacc("TRN2", target_bir_lowering=False, num_devices=1)
    aps = {n: nc.dram_tensor(f"in_{n}", v.shape, mybir.dt.from_np(v.dtype), kind="ExternalInput").ap()
           for n, v in arrays.items()}
    aps["out"] = nc.dram_tensor("out_0", (N, D), F32, kind="ExternalOutput").ap()
    build(nc, aps)
    r = run_bass_kernel_spmd(nc, [{f"in_{n}": v for n, v in arrays.items()}], core_ids=[0])
    return r.results[0]["out_0"]
```

```python
from contextlib import ExitStack

import numpy as np
import concourse.bass as bass
from concourse import mybir

F32, F32R, I32, BF16 = mybir.dt.float32, mybir.dt.float32r, mybir.dt.int32, mybir.dt.bfloat16
ALU = mybir.AluOpType
ACT = mybir.ActivationFunctionType
AX_X = mybir.AxisListType.X

P = 128
N, E, D, ED = 12500, 212500, 128, 16
EPS = 1e-5
GROUP_TILES = 8
GROUP_EDGES = GROUP_TILES * P
GROUPS = -(-E // GROUP_EDGES)
TILES = GROUPS * GROUP_TILES
WINDOW = 96
ROUNDS_ALL = -(-N // WINDOW)
NT = ROUNDS_ALL * WINDOW + WINDOW
NO_NODE = 1 << 20
PAIR = 2
PARTS = 4
BODY = 4
BODIES = GROUPS // BODY
GROUP_COLS = GROUP_EDGES // PAIR
GRAM_COLS, GRAM_SLOTS = 1024, 4
GRAM_LOADS = TILES * ED // GRAM_COLS
GRAM_BODIES = GRAM_LOADS // GRAM_SLOTS
GRAM_REST = GRAM_LOADS % GRAM_SLOTS
CHUNK = 512
CHUNKS = N // CHUNK
TAIL = N - CHUNKS * CHUNK
PER = 4
BASE_ROWS = GROUPS // 2

assert GROUPS % BODY == 0 and TILES * ED % GRAM_COLS == 0 and CHUNKS % 8 == 0 and TAIL % PER == 0


def wait(engine, semaphore, value):
    if isinstance(value, int) and value <= 0:
        return
    engine.wait_ge(semaphore, value)


def build(nc, a):
    with ExitStack() as ctx:
        def sb(name, shape, dt=F32):
            return ctx.enter_context(nc.sbuf_tensor(name, shape, dt))

        def sem(name):
            return ctx.enter_context(nc.semaphore(name))

        table = sb("table", [P, 2, NT])
        rows = sb("rows", [P, 4, GROUP_TILES * D])
        onehot = sb("onehot", [P, 2, GROUP_TILES, WINDOW])
        ea = sb("ea", [P, 2, 2 * GROUP_COLS])
        ea_high = sb("ea_high", [P, 2, GROUP_COLS], F32R)
        ea_parts = sb("ea_parts", [P, 2, GROUP_COLS], F32R)
        dst_i = sb("dst_i", [P, TILES], I32)
        dst_f = sb("dst_f", [P, TILES])
        rel = sb("rel", [P, TILES])
        idx = sb("idx", [P, 2, 2 * GROUP_TILES], I32)
        iota = sb("iota_sb", [P, WINDOW])
        ident = sb("ident_sb", [P, P])
        block_mask = sb("block_mask_sb", [P, P])
        fold = sb("fold_sb", [P, ED])
        ones = sb("ones", [P, P])
        eps = sb("eps", [P, 1])
        act_warm = sb("act_warm", [P, 1])
        ones_bf = sb("ones_bf", [P, P], BF16)
        ee_w1bd = sb("ee_w1bd_sb", [P, PAIR * D])
        ee_w1f = sb("ee_w1f", [P, PAIR * D])
        ee_w1high = sb("ee_w1high", [P, PAIR * D], F32R)
        ee_w1parts = sb("ee_w1parts", [P, PAIR * D], F32R)
        ee_shift = sb("ee_shift", [P, D])
        ee_negshift = sb("ee_negshift", [P, D])
        shift_col = sb("shift_col", [P, 1])
        per_edge = sb("per_edge", [P, 1])
        low_rows = sb("low_rows_sb", [P, 2])
        ee_w1 = sb("ee_w1_sb", [ED, D])
        ee_w2 = sb("ee_w2_sb", [D, D])
        mlp_w1 = sb("mlp_w1_sb", [D, D])
        mlp_w2 = sb("mlp_w2_sb", [D, D])
        rowvec = sb("rowvec", [P, 3, D])
        colvec = sb("colvec", [P, 7])
        stage_x = sb("stage_x", [P, 4, CHUNK])
        part = sb("part", [P, GRAM_LOADS, ED])
        part1 = sb("part1", [P, ED])
        gram = sb("gram", [P, P])
        gram1 = sb("gram1", [P, ED])
        mean_row = sb("mean_row", [1, ED])
        mean_col = sb("mean_col", [ED, 1])
        cov = sb("cov", [ED, ED])
        cov1 = sb("cov1", [ED, ED])
        prod = sb("prod", [ED, 2, D])
        bnrow = sb("bnrow", [P, 5, D])
        base_min = sb("base_min", [BASE_ROWS, 2])
        base0 = sb("base0", [P, GROUPS])
        base = sb("base", [P, GROUPS])
        base_i = sb("base_i", [1, GROUPS], I32)
        wide = sb("wide", [P, 4])
        rounds_i = sb("rounds_i", [1, 1], I32)
        bn_parts = sb("bn_parts", [P, CHUNKS + 1, 6])
        bn_out = sb("bn_out", [P, 2, 2])
        bn_col = sb("bn_col", [P, 2, 4])
        summed = sb("summed", [P, 2, CHUNK])
        ln_parts = sb("ln_parts", [P, 8, PER, 6])
        ln_out = sb("ln_out", [P, 8, PER, 2])
        ln_root = sb("ln_root", [P, 8, PER])
        ln_rstd = sb("ln_rstd", [P, 8, 2, PER])
        ps = ctx.enter_context(nc.psum_tensor("ps", [P, 8, 512], F32))

        base_dram = nc.dram_tensor("base_scratch", (GROUPS,), F32, kind="Internal").ap()
        h_dram = nc.dram_tensor("h_scratch", (N, D), F32, kind="Internal").ap()

        weights_in, dst_in, groups_in, base_out, base_in = (
            sem(n) for n in ("weights_in", "dst_in", "groups_in", "base_out", "base_in"))
        gram_in = [sem(f"gram_in{s}") for s in range(GRAM_SLOTS)]
        gram_summed, gram_done = sem("gram_summed"), sem("gram_done")
        base_ready, step, pe_step, cleared = sem("base_ready"), sem("step"), sem("pe_step"), sem("cleared")
        root_ready, checked = sem("root_ready"), sem("checked")
        WEIGHTS = 13 + 7

        def rewind(dve):
            dve.tensor_scalar(base[:], base0[:], wide[:, 2:3], None, ALU.mult)

        with nc.Block() as block:
            @block.sync
            def _(sp):
                def load(s, n):
                    sp.dma_start(rows[:, s, 0:GRAM_COLS],
                                 a["edges"][:, bass.ds(n * GRAM_COLS, GRAM_COLS)]).then_inc(gram_in[s], 16)
                def reload(s, i):
                    sp.wait_ge(gram_done, i * GRAM_SLOTS + (s + 1 - GRAM_SLOTS))
                    sp.wait_ge(gram_summed, i * GRAM_SLOTS + (s + 1 - GRAM_SLOTS))
                    load(s, i * GRAM_SLOTS + s)

                for s in range(GRAM_SLOTS):
                    load(s, s)
                sp.dma_start(table[0:BASE_ROWS, 1, 0:2 * GROUP_EDGES].bitcast(I32),
                             a["dst_groups"].rearrange("(r two) e -> r (two e)", two=2)).then_inc(groups_in, 16)
                sp.dma_start(dst_i[:], a["dst_tiles"]).then_inc(dst_in, 16)
                with sp.Fori(1, GRAM_BODIES) as i:
                    for s in range(GRAM_SLOTS):
                        reload(s, i)
                for s in range(GRAM_REST):
                    reload(s, GRAM_BODIES)

            @block.scalar
            def _(act):
                for t, n in ((ident, "ident"), (iota, "iota"), (block_mask, "block_mask"), (fold, "fold"),
                             (ee_w1bd, "ee_w1bd"), (low_rows, "low_rows"), (ee_w1, "ee_w1"), (ee_w2, "ee_w2"),
                             (mlp_w1, "mlp_w1"), (mlp_w2, "mlp_w2")):
                    act.dma_start(t[:], a[n]).then_inc(weights_in, 16)
                for k, n in enumerate(("ee_b1", "ee_g1", "ee_bb1")):
                    act.dma_start(rowvec[:, k, :], a[n].rearrange("(o d) -> o d", o=1).broadcast_to([P, D])
                                  ).then_inc(weights_in, 16)
                for k, n in enumerate(("ee_b2", "mlp_b1", "mlp_g1", "mlp_bb1", "mlp_b2", "mlp_g2", "mlp_bb2")):
                    act.dma_start(colvec[:, k:k + 1], a[n].rearrange("(d o) -> d o", o=1)).then_inc(weights_in, 16)
                act.wait_ge(cleared, 1)
                act.activation(act_warm[:], eps[:], ACT.Sqrt)
                act.wait_ge(base_ready, 1)
                act.dma_start(base_dram.rearrange("(r two) -> r two", two=2), base_min[:]).then_inc(base_out, 16)
                act.wait_ge(base_out, 16)
                act.dma_start(base0[:], base_dram.rearrange("(o g) -> o g", o=1).broadcast_to([P, GROUPS])
                              ).then_inc(base_in, 16)
                act.wait_ge(pe_step, 4)
                act.activation(bnrow[:, 2, :], ps[:, 7, 0:D], ACT.Sqrt, bias=eps[:]).then_inc(root_ready, 1)

            @block.gpsimd
            def _(pool):
                pool.memset(eps[:], EPS).then_inc(cleared, 1)
                pool.memset(ones[:], 1.0).then_inc(cleared, 1)
                pool.memset(ones_bf[:], 1.0).then_inc(cleared, 1)
                pool.memset(table[:, 0, :], 0.0).then_inc(cleared, 1)
                pool.wait_ge(base_ready, 1)
                pool.memset(table[:, 1, :], 0.0).then_inc(cleared, 1)
                pool.wait_ge(base_in, 16)
                pool.wait_ge(base_ready, 2)
                grouped = rel[:].rearrange("p (g t) -> p g t", t=GROUP_TILES)
                pool.tensor_tensor(grouped, dst_f[:].rearrange("p (g t) -> p g t", t=GROUP_TILES),
                                   base0[:].unsqueeze(2).broadcast_to([P, GROUPS, GROUP_TILES]), ALU.subtract
                                   ).then_inc(checked, 1)
                pool.wait_ge(checked, 1)
                pool.tensor_scalar(dst_i[:].bitcast(F32), rel[:], NO_NODE / 2.0, None, ALU.is_lt).then_inc(checked, 1)
                pool.wait_ge(checked, 2)
                pool.tensor_scalar(rel[:], rel[:], float(WINDOW), None, ALU.is_ge).then_inc(checked, 1)
                pool.wait_ge(checked, 3)
                pool.tensor_tensor(rel[:], rel[:], dst_i[:].bitcast(F32), ALU.mult).then_inc(checked, 1)

            @block.tensor
            def _(pe):
                def gram_slot(n, s, i):
                    pe.wait_ge(gram_in[s], 16 * (i + 1))
                    for b in range(GRAM_COLS // P):
                        x = rows[:, s, b * P:(b + 1) * P]
                        mm = pe.matmul(ps[:, 0, 0:P], x, x, start=(n == 0 and b == 0), stop=True,
                                       skip_group_check=True)
                    mm.then_inc(gram_done, 1)
                for s in range(GRAM_SLOTS):
                    gram_slot(s, s, 0)
                with pe.Fori(1, GRAM_BODIES) as i:
                    for s in range(GRAM_SLOTS):
                        gram_slot(None, s, i)
                for s in range(GRAM_REST):
                    gram_slot(None, s, GRAM_BODIES)
                pe.wait_ge(cleared, 2)
                pe.wait_ge(step, 2)
                pe.wait_ge(weights_in, 16 * WEIGHTS)
                pe.matmul(ps[0:1, 1, 0:ED], ones[:, 0:1], part1[:], start=True, stop=True)
                pe.matmul(ps[0:ED, 2, 0:1], part1[:], ones[:, 0:1], start=True, stop=True)
                pe.matmul(ps[:, 2, 8:9], ones[:], wide[:, 0:1], start=True, stop=True)
                pe.matmul(ps[:, 3, 0:ED], gram[:], fold[:], start=True, stop=True).then_inc(pe_step, 1)
                pe.wait_ge(step, 5)
                pe.matmul(ps[0:ED, 4, 0:ED], fold[:], gram1[:], start=True, stop=True)
                pe.matmul(ps[0:ED, 5, 0:ED], mean_row[:], mean_row[:], start=True, stop=True).then_inc(pe_step, 1)
                pe.wait_ge(step, 7)
                pe.matmul(ps[0:ED, 6, 0:D], cov[:], ee_w1[:], start=True, stop=True).then_inc(pe_step, 1)
                pe.wait_ge(step, 9)
                pe.matmul(ps[:, 7, 0:D], ones[0:ED, :], prod[:, 0, :], start=True, stop=True)
                pe.matmul(ps[:, 7, D:2 * D], ones[0:ED, :], prod[:, 1, :], start=True, stop=True
                          ).then_inc(pe_step, 1)
                pe.wait_ge(step, 15)
                pe.matmul(ps[:, 0, 0:1], ee_shift[0:1, :], ones[0:1, 0:1], start=True, stop=True).then_inc(pe_step, 1)
                pe.wait_ge(step, 18)
                pe.matmul(ps[:, 1, 0:1], ee_w2[:], shift_col[:], start=True, stop=True).then_inc(pe_step, 1)

            @block.vector
            def _(dve):
                steps = [0]

                def link(ins):
                    steps[0] += 1
                    ins.then_inc(step, 1)
                    dve.wait_ge(step, steps[0])

                def sum_slot(s, i):
                    dve.wait_ge(gram_in[s], 16 * (i + 1))
                    dve.tensor_reduce(part[:, bass.ds(i * GRAM_SLOTS + s, 1), :],
                                      rows[:, s, 0:GRAM_COLS].rearrange("p (n c) -> p c n", c=ED),
                                      AX_X, ALU.add).then_inc(gram_summed, 1)
                for s in range(GRAM_SLOTS):
                    sum_slot(s, 0)
                dve.wait_ge(groups_in, 16)
                dve.tensor_reduce(base_min[:], table[0:BASE_ROWS, 1, 0:2 * GROUP_EDGES].bitcast(I32)
                                  .rearrange("r (two e) -> r two e", two=2), AX_X, ALU.min).then_inc(base_ready, 1)
                dve.wait_ge(dst_in, 16)
                dve.tensor_copy(dst_f[:], dst_i[:]).then_inc(base_ready, 1)
                with dve.Fori(1, GRAM_BODIES) as i:
                    for s in range(GRAM_SLOTS):
                        sum_slot(s, i)
                for s in range(GRAM_REST):
                    sum_slot(s, GRAM_BODIES)
                dve.wait_ge(gram_summed, GRAM_LOADS)
                dve.wait_ge(checked, 4)
                dve.tensor_reduce(wide[:, 0:1], rel[:], AX_X, ALU.max)
                link(dve.tensor_reduce(part1[:], part[:].rearrange("p n c -> p c n"), AX_X, ALU.add))
                dve.wait_ge(gram_done, GRAM_LOADS)
                dve.wait_ge(weights_in, 16 * WEIGHTS)
                link(dve.tensor_tensor(gram[:], ps[:, 0, 0:P], block_mask[:], ALU.mult))
                dve.wait_ge(pe_step, 1)
                link(dve.tensor_scalar(mean_row[:], ps[0:1, 1, 0:ED], 1.0 / E, None, ALU.mult))
                link(dve.tensor_scalar(mean_col[:], ps[0:ED, 2, 0:1], 1.0 / E, None, ALU.mult))
                link(dve.tensor_copy(gram1[:], ps[:, 3, 0:ED]))
                dve.wait_ge(pe_step, 2)
                link(dve.tensor_scalar(cov1[:], ps[0:ED, 4, 0:ED], 1.0 / E, None, ALU.mult))
                link(dve.tensor_tensor(cov[:], cov1[:], ps[0:ED, 5, 0:ED], ALU.subtract))
                dve.wait_ge(pe_step, 3)
                link(dve.tensor_tensor(prod[:, 0, :], ps[0:ED, 6, 0:D], ee_w1[:], ALU.mult))
                link(dve.tensor_scalar(prod[:, 1, :], ee_w1[:], mean_col[:, 0:1], None, ALU.mult))
                dve.wait_ge(pe_step, 4)
                dve.wait_ge(root_ready, 1)
                link(dve.reciprocal(bnrow[:, 0, :], bnrow[:, 2, :]))
                link(dve.tensor_tensor(bnrow[:, 1, :], bnrow[:, 0, :], rowvec[:, 1, :], ALU.mult))
                link(dve.tensor_tensor(bnrow[:, 2, :], ps[:, 7, D:2 * D], rowvec[:, 0, :], ALU.add))
                link(dve.tensor_tensor(bnrow[:, 3, :], rowvec[:, 0, :], bnrow[:, 2, :], ALU.subtract))
                link(dve.tensor_tensor(bnrow[:, 4, :], bnrow[:, 3, :], bnrow[:, 1, :], ALU.mult))
                link(dve.tensor_tensor(ee_shift[:], bnrow[:, 4, :], rowvec[:, 2, :], ALU.add))
                dve.tensor_scalar(ee_negshift[:], ee_shift[:], -1.0, None, ALU.mult)
                link(dve.tensor_tensor(ee_w1f[:].rearrange("r (q d) -> r q d", q=PAIR),
                                       ee_w1bd[:].rearrange("r (q d) -> r q d", q=PAIR),
                                       bnrow[:, 1:2, :].broadcast_to([P, PAIR, D]), ALU.mult))
                link(dve.tensor_scalar(ee_w1high[:], ee_w1f[:], low_rows[:, 1:2], None, ALU.mult))
                dve.tensor_tensor(ee_w1parts[:], ee_w1f[:], ee_w1high[:].bitcast(F32), ALU.subtract)
                dve.wait_ge(pe_step, 5)
                link(dve.tensor_copy(shift_col[:], ps[:, 0, 0:1]))
                dve.wait_ge(pe_step, 6)
                link(dve.tensor_tensor(per_edge[:], ps[:, 1, 0:1], colvec[:, 0:1], ALU.add))
                link(dve.tensor_scalar(wide[:, 1:2], ps[:, 2, 8:9], 0.5, None, ALU.is_ge))
                link(dve.tensor_scalar(wide[:, 2:3], wide[:, 1:2], -1.0, 1.0, ALU.mult, ALU.add))
                link(dve.tensor_scalar(rounds_i[:], wide[0:1, 1:2], float(ROUNDS_ALL - 1), 1.0, ALU.mult, ALU.add))
                rewind(dve)

        ea_in = [sem("ea_in0"), sem("ea_in1")]
        high_done, parts_done, features_done, clamped, onehot_done, sums_done, added = (
            sem(n) for n in ("high_done", "parts_done", "features_done", "clamped", "onehot_done", "sums_done", "added"))
        idx_in = [sem("idx_in0"), sem("idx_in1")]
        gathering = sem("gathering")
        gathered = [sem(f"gathered{s}") for s in range(4)]
        round_sems = [*ea_in, high_done, parts_done, features_done, clamped, onehot_done, sums_done, added,
                      *idx_in, gathering, *gathered]

        def open_round():
            with nc.Block() as block:
                @block.gpsimd
                def _(pool):
                    for s in round_sems:
                        pool.sem_clear(s)

                @block.vector
                def _(dve):
                    dve.tensor_tensor(rel[:].rearrange("p (g t) -> p g t", t=GROUP_TILES),
                                      dst_f[:].rearrange("p (g t) -> p g t", t=GROUP_TILES),
                                      base[:].unsqueeze(2).broadcast_to([P, GROUPS, GROUP_TILES]), ALU.subtract)
                    dve.tensor_copy(base_i[:], base[0:1, :])

        def window_sums(dve, kinds):
            def make_onehot(g, u):
                wait(dve, sums_done, g - 1)
                dve.tensor_tensor(onehot[:, u % 2],
                                  iota[:].unsqueeze(1).broadcast_to([P, GROUP_TILES, WINDOW]),
                                  rel[:, bass.ds(g * GROUP_TILES, GROUP_TILES)].unsqueeze(2)
                                  .broadcast_to([P, GROUP_TILES, WINDOW]), ALU.is_equal).then_inc(onehot_done, 1)

            def clamp(g, u):
                dve.wait_ge(features_done, g + 1)
                wait(dve, sums_done, g - 1)
                b = 2 * (u % 2)
                dve.tensor_tensor(rows[:, u % 2, :].rearrange("p (t d) -> p t d", d=D),
                                  ps[:, b:b + 2, :].rearrange("p b (t d) -> p (b t) d", d=D),
                                  ee_negshift[:].unsqueeze(1).broadcast_to([P, GROUP_TILES, D]), ALU.max
                                  ).then_inc(clamped, 1)

            def add_window(g, u):
                at = dve.value_load(base_i[0:1, bass.ds(g, 1)], min_val=0, max_val=NT - WINDOW)
                dve.wait_ge(sums_done, g + 1)
                wait(dve, added, g)
                here = table[:, 0:kinds, bass.ds(at, WINDOW)]
                dve.tensor_tensor(here, here, ps[:, 4 + 2 * (u % 2):4 + 2 * (u % 2) + kinds, 0:WINDOW], ALU.add
                                  ).then_inc(added, 1)

            def body(i, last=False):
                for u in range(BODY):
                    if not (last and u == BODY - 1):
                        make_onehot(i * BODY + u + 1, u + 1)
                        if kinds == 2:
                            clamp(i * BODY + u + 1, u + 1)
                    add_window(i * BODY + u, u)

            make_onehot(0, 0)
            if kinds == 2:
                clamp(0, 0)
            body(0)
            with dve.Fori(1, BODIES - 1) as i:
                body(i)
            body(BODIES - 1, last=True)
            dve.tensor_scalar(base[:], base[:], float(WINDOW), None, ALU.add)

        nc.all_engine_barrier()
        rounds = nc.values_load(rounds_i[0:1, 0:1], min_val=1, max_val=ROUNDS_ALL)
        with nc.Fori(0, rounds):
            open_round()
            with nc.Block() as block:
                @block.sync
                def _(sp):
                    def load(i, s):
                        for part in range(PARTS):
                            sp.dma_start(ea[part * PAIR * ED:(part + 1) * PAIR * ED, s, :],
                                         a["edges_t"][:, bass.ds((i * 2 + s) * 2 * GROUP_COLS, 2 * GROUP_COLS)]
                                         ).then_inc(ea_in[s], 16)
                    load(0, 0)
                    load(0, 1)
                    with sp.Fori(1, BODIES) as i:
                        for s in range(2):
                            sp.wait_ge(parts_done, i * BODY + (2 * s - 2))
                            load(i, s)

                @block.scalar
                def _(act):
                    def high(i, u):
                        if u % 2 == 0:
                            act.wait_ge(ea_in[u // 2], 16 * PARTS * (i + 1))
                        wait(act, parts_done, i * BODY + (u - 1))
                        act.activation(ea_high[:, u % 2, :], ea[:, u // 2, (u % 2) * GROUP_COLS:(u % 2 + 1) * GROUP_COLS],
                                       ACT.Copy, scale=low_rows[:, 0:1]).then_inc(high_done, 1)
                    for u in range(BODY):
                        high(0, u)
                    with act.Fori(1, BODIES) as i:
                        for u in range(BODY):
                            high(i, u)

                @block.gpsimd
                def _(pool):
                    def split(i, u):
                        wait(pool, features_done, i * BODY + (u - 1))
                        pool.wait_ge(high_done, i * BODY + u + 1)
                        pool.tensor_tensor(ea_parts[:, u % 2, :],
                                           ea[:, u // 2, (u % 2) * GROUP_COLS:(u % 2 + 1) * GROUP_COLS],
                                           ea_high[:, u % 2, :].bitcast(F32), ALU.subtract).then_inc(parts_done, 1)
                    for u in range(BODY):
                        split(0, u)
                    with pool.Fori(1, BODIES) as i:
                        for u in range(BODY):
                            split(i, u)

                @block.tensor
                def _(pe):
                    def features(g, u):
                        wait(pe, clamped, g - 1)
                        pe.wait_ge(parts_done, g + 1)
                        for pair in range(GROUP_TILES // PAIR):
                            mm = pe.matmul(ps[:, 2 * (u % 2) + pair // 2, (pair % 2) * PAIR * D:(pair % 2 + 1) * PAIR * D],
                                           ea_parts[:, u % 2, pair * P:(pair + 1) * P], ee_w1parts[:],
                                           start=True, stop=True)
                        mm.then_inc(features_done, 1)

                    def sums(g, u):
                        wait(pe, added, g - 1)
                        pe.wait_ge(onehot_done, g + 1)
                        for t in range(GROUP_TILES):
                            pe.matmul(ps[:, 5 + 2 * (u % 2), 0:WINDOW], ones_bf[:],
                                      onehot[:, u % 2, t, :].bitcast(BF16)[:, 1:2 * WINDOW:2],
                                      start=(t == 0), stop=(t == GROUP_TILES - 1))
                        pe.wait_ge(clamped, g + 1)
                        for t in range(GROUP_TILES):
                            mm = pe.matmul(ps[:, 4 + 2 * (u % 2), 0:WINDOW], rows[:, u % 2, t * D:(t + 1) * D],
                                           onehot[:, u % 2, t, :], start=(t == 0), stop=(t == GROUP_TILES - 1))
                        mm.then_inc(sums_done, 1)

                    def body(i, last=False):
                        for u in range(BODY):
                            g = i * BODY + u
                            if not (last and u == BODY - 1):
                                features(g + 1, u + 1)
                            sums(g, u)

                    features(0, 0)
                    body(0)
                    with pe.Fori(1, BODIES - 1) as i:
                        body(i)
                    body(BODIES - 1, last=True)

                @block.vector
                def _(dve):
                    window_sums(dve, kinds=2)

        x_in, h_out = ([sem(f"{n}{s}") for s in range(4)] for n in ("x_in", "h_out"))
        projected, h_half, h_ready, h_kept, turned, h_copied = (
            sem(n) for n in ("projected", "h_half", "h_ready", "h_kept", "turned", "h_copied"))
        staged_h, staged_rows = rows[:, :, 0:CHUNK], rows[:, :, CHUNK:2 * CHUNK]

        def over_chunks(engine, step_of, slots=2):
            for s in range(slots):
                step_of(s, s, CHUNK)
            with engine.Fori(1, CHUNKS // slots) as i:
                for s in range(slots):
                    step_of(i * slots + s, s, CHUNK)
            step_of(CHUNKS, CHUNKS % slots, TAIL)

        def between(c, s, n):
            pass

        def lagging(engine, stages, slots):
            def step_of(c, s, n):
                for k, stage in enumerate(stages):
                    if isinstance(c, int) and c < k:
                        break
                    stage(c - k, (s - k) % slots, n if k == 0 else CHUNK)
            over_chunks(engine, step_of, slots=slots)
            for late in range(1, len(stages)):
                for k in range(late, len(stages)):
                    c = CHUNKS + late - k
                    stages[k](c, c % slots, TAIL if c == CHUNKS else CHUNK)

        def uses(c, s, slots=2):
            return (c // slots) * 16 if isinstance(c, int) else (c - s) * (16 // slots)

        def by_parity(c, s):
            return c + 2 - s % 2

        def turn(pe, bank, source, n):
            for k in range(PER):
                tr = pe.transpose(ps[0:n // PER, bank, k * D:(k + 1) * D], source[:, k:n:PER], ident[:])
            return tr

        def rows_of(dram, c, n):
            return dram[bass.ds(c * CHUNK, n), :].rearrange("(p k) d -> p (k d)", k=PER)

        with nc.Block() as block:
            @block.sync
            def _(sp):
                def load(c, s, n):
                    wait(sp, h_ready, c - 3)
                    sp.dma_start(stage_x[:, s % 4, 0:n], a["x_t"][:, bass.ds(c * CHUNK, n)]).then_inc(x_in[s % 4], 16)

                def store(c, s, n):
                    sp.wait_ge(h_copied, c + 1)
                    sp.dma_start(rows_of(h_dram, c, n), staged_rows[0:n // PER, s % 4, :]).then_inc(h_out[s % 4], 16)
                lagging(sp, [load] + 4 * [between] + [store], slots=8)
                for s in range(4):
                    sp.wait_ge(h_out[s], 16 * (CHUNKS // 4 + (s == 0)))

            @block.tensor
            def _(pe):
                def project(c, s, n):
                    wait(pe, h_half, c - 3)
                    pe.matmul(ps[:, s % 4, 0:n], ee_w2[:], table[:, 0, bass.ds(c * CHUNK, n)], start=True, stop=True
                              ).then_inc(projected, 1)

                def turn_h(c, s, n):
                    pe.wait_ge(h_ready, c + 1)
                    wait(pe, h_copied, c - 3)
                    turn(pe, 4 + s % 4, staged_h[:, s % 4, :], n).then_inc(turned, 1)
                lagging(pe, [project, between, turn_h], slots=8)

            @block.vector
            def _(dve):
                def combine(c, s, n):
                    dve.wait_ge(projected, c + 1)
                    wait(dve, turned, c - 3)
                    wait(dve, h_kept, c - 3)
                    dve.scalar_tensor_tensor(staged_h[:, s % 4, 0:n], table[:, 1, bass.ds(c * CHUNK, n)],
                                             per_edge[:, 0:1], ps[:, s % 4, 0:n], ALU.mult, ALU.add
                                             ).then_inc(h_half, 1)

                def add_x(c, s, n):
                    dve.wait_ge(x_in[s % 4], uses(c, s % 4, 4) + 16)
                    dve.wait_ge(h_half, c + 1)
                    dve.tensor_tensor(staged_h[:, s % 4, 0:n], staged_h[:, s % 4, 0:n], stage_x[:, s % 4, 0:n], ALU.add
                                      ).then_inc(h_ready, 1)
                lagging(dve, [combine, add_x], slots=8)
                rewind(dve)

            @block.scalar
            def _(act):
                def keep(c, s, n):
                    act.wait_ge(h_ready, c + 1)
                    act.copy(table[:, 0, bass.ds(c * CHUNK, n)], staged_h[:, s % 4, 0:n]).then_inc(h_kept, 1)

                def copy_rows(c, s, n):
                    act.wait_ge(turned, c + 1)
                    wait(act, h_out[s % 4], uses(c, s % 4, 4))
                    act.copy(staged_rows[0:n // PER, s % 4, :], ps[0:n // PER, 4 + s % 4, :]).then_inc(h_copied, 1)
                lagging(act, [keep, between, copy_rows], slots=8)

        with nc.Fori(0, rounds):
            open_round()
            with nc.Block() as block:
                @block.sync
                def _(sp):
                    def load(i, s):
                        sp.dma_start(idx[:, s, :], a["src_tiles"][:, bass.ds((i * 2 + s) * 2 * GROUP_TILES,
                                                                             2 * GROUP_TILES)]).then_inc(idx_in[s], 16)
                    load(0, 0)
                    load(0, 1)
                    with sp.Fori(1, BODIES) as i:
                        for s in range(2):
                            sp.wait_ge(gathered[2 * s], i * (16 * GROUP_TILES))
                            sp.wait_ge(gathered[2 * s + 1], i * (16 * GROUP_TILES))
                            load(i, s)

                @block.gpsimd
                def _(pool):
                    def body(i):
                        for u in range(BODY):
                            if u % 2 == 0:
                                pool.wait_ge(idx_in[u // 2], 16 * (i + 1))
                            wait(pool, sums_done, i * BODY + (u - 3))
                            pool.sem_inc(gathering, 1)
                            for t in range(GROUP_TILES):
                                k = (u % 2) * GROUP_TILES + t
                                pool.indirect_dma_start(
                                    rows[:, u, t * D:(t + 1) * D], None, h_dram,
                                    bass.IndirectOffsetOnAxis(ap=idx[:, u // 2, k:k + 1], axis=0)
                                ).then_inc(gathered[u], 16)
                    body(0)
                    with pool.Fori(1, BODIES) as i:
                        body(i)

                @block.tensor
                def _(pe):
                    def body(i):
                        for u in range(BODY):
                            g = i * BODY + u
                            wait(pe, added, g - 1)
                            pe.wait_ge(onehot_done, g + 1)
                            pe.wait_ge(gathered[u], (i + 1) * (16 * GROUP_TILES))
                            for t in range(GROUP_TILES):
                                mm = pe.matmul(ps[:, 4 + 2 * (u % 2), 0:WINDOW], rows[:, u, t * D:(t + 1) * D],
                                               onehot[:, u % 2, t, :], start=(t == 0), stop=(t == GROUP_TILES - 1))
                            mm.then_inc(sums_done, 1)
                    body(0)
                    with pe.Fori(1, BODIES) as i:
                        body(i)

                @block.vector
                def _(dve):
                    window_sums(dve, kinds=1)

        made, stats, ready, bn_root = ([sem(f"{n}{k}") for k in range(2)]
                                       for n in ("made", "stats", "bn_ready", "bn_root"))
        kept = [[sem(f"kept{k}_even"), sem(f"kept{k}_odd")] for k in range(2)]
        relued = sem("relued")
        z, y1, y2 = table[:, 0], table[:, 1], table[:, 0]
        BANKS = 8
        staged_out, staged_relu = rows[:, :, 0:CHUNK], rows[:, :, CHUNK:2 * CHUNK]
        for layer in range(2):
            weight, bias = (mlp_w1, 1) if layer == 0 else (mlp_w2, 4)
            source, out = (z, y1) if layer == 0 else (y1, y2)
            with nc.Block() as block:
                @block.tensor
                def _(pe, layer=layer, weight=weight, source=source):
                    def dense(c, s, n):
                        wait(pe, kept[layer][s % 2], by_parity(c - BANKS, s))
                        if layer:
                            pe.wait_ge(relued, c + 1)
                        moving = staged_relu[:, s % 4, 0:n] if layer else source[:, bass.ds(c * CHUNK, n)]
                        pe.matmul(ps[:, s, 0:n], weight[:], moving, start=True, stop=True).then_inc(made[layer], 1)
                    over_chunks(pe, dense, slots=BANKS)

                @block.scalar
                def _(act, layer=layer, bias=bias, source=source, out=out):
                    def relu(c, s, n):
                        wait(act, made[1], c - 3)
                        act.activation(staged_relu[:, s % 4, 0:n], source[:, bass.ds(c * CHUNK, n)], ACT.Relu,
                                       bias=bn_col[:, 0, 3:4], scale=bn_col[:, 0, 1:2]).then_inc(relued, 1)

                    def keep(c, s, n):
                        if layer and s % 2:
                            return
                        act.wait_ge(made[layer], c + 1)
                        act.activation(out[:, bass.ds(c * CHUNK, n)], ps[:, s, 0:n], ACT.Identity,
                                       bias=colvec[:, bias:bias + 1]).then_inc(kept[layer][s % 2], 2)
                    lagging(act, [relu, between, keep] if layer else [keep], slots=BANKS)
                    act.wait_ge(ready[layer], 1)
                    act.activation(bn_col[:, layer, 2:3], bn_out[:, layer, 1:2], ACT.Sqrt, bias=eps[:]
                                   ).then_inc(bn_root[layer], 1)

                @block.vector
                def _(dve, layer=layer, bias=bias, out=out):
                    def keep(c, s, n):
                        if s % 2 == 0:
                            return
                        dve.wait_ge(made[layer], c + 1)
                        dve.tensor_scalar(out[:, bass.ds(c * CHUNK, n)], ps[:, s, 0:n],
                                          colvec[:, bias:bias + 1], None, ALU.add).then_inc(kept[layer][1], 2)

                    def measure(c, s, n):
                        dve.wait_ge(kept[layer][s % 2], by_parity(c, s))
                        dve.bn_stats(bn_parts[:, bass.ds(c, 1), :].rearrange("p o s -> p (o s)"),
                                     out[:, bass.ds(c * CHUNK, n)]).then_inc(stats[layer], 1)
                    lagging(dve, [keep, measure] if layer else [measure], slots=BANKS)
                    dve.wait_ge(stats[layer], CHUNKS + 1)
                    k = [0]

                    def link(ins):
                        k[0] += 1
                        ins.then_inc(ready[layer], 1)
                        dve.wait_ge(ready[layer], k[0])
                    link(dve.bn_aggr(bn_out[:, layer, :], bn_parts[:]))
                    dve.wait_ge(bn_root[layer], 1)
                    link(dve.reciprocal(bn_col[:, layer, 0:1], bn_col[:, layer, 2:3]))
                    link(dve.tensor_tensor(bn_col[:, layer, 1:2], bn_col[:, layer, 0:1],
                                           colvec[:, bias + 1:bias + 2], ALU.mult))
                    link(dve.tensor_tensor(bn_col[:, layer, 2:3], bn_out[:, layer, 0:1],
                                           bn_col[:, layer, 1:2], ALU.mult))
                    link(dve.tensor_tensor(bn_col[:, layer, 3:4], colvec[:, bias + 2:bias + 3],
                                           bn_col[:, layer, 2:3], ALU.subtract))

        xr_in, out_done = ([sem(f"{n}{s}") for s in range(4)] for n in ("xr_in", "out"))
        relu2, residual, turned2, ln_stat, measured, rooted, ln_ready = (
            sem(n) for n in ("relu2", "residual", "turned2", "ln_stat", "measured", "rooted", "ln_ready"))
        normed = [sem("normed_even"), sem("normed_odd")]
        ln_inverse, aggregating = sem("ln_inverse"), sem("aggregating")
        with nc.Block() as block:
            @block.sync
            def _(sp):
                def load(c, s, n):
                    wait(sp, residual, c - 3)
                    sp.dma_start(stage_x[:, s % 4, 0:n], a["x_t"][:, bass.ds(c * CHUNK, n)]).then_inc(xr_in[s % 4], 16)

                def store(c, s, n):
                    sp.wait_ge(normed[s % 2], by_parity(c, s))
                    sp.dma_start(rows_of(a["out"], c, n), staged_out[0:n // PER, s % 4, :]).then_inc(out_done[s % 4], 16)
                for s in range(4):
                    sp.sem_inc(out_done[s], 16)
                lagging(sp, [load] + 7 * [between] + [store], BANKS)
                for s in range(4):
                    sp.wait_ge(out_done[s], 16 * (1 + CHUNKS // 4 + (s == 0)))

            @block.gpsimd
            def _(pool):
                def add_x(c, s, n):
                    pool.wait_ge(relu2, c + 1)
                    pool.wait_ge(xr_in[s % 4], uses(c, s % 4, 4) + 16)
                    wait(pool, turned2, c - 1)
                    pool.tensor_tensor(summed[:, s % 2, 0:n], staged_relu[:, s % 4, 0:n], stage_x[:, s % 4, 0:n], ALU.add
                                       ).then_inc(residual, 1)
                over_chunks(pool, add_x, slots=BANKS)

            @block.tensor
            def _(pe):
                def to_rows(c, s, n):
                    pe.wait_ge(residual, c + 1)
                    wait(pe, normed[s % 2], by_parity(c - BANKS, s))
                    turn(pe, s, summed[:, s % 2, :], n).then_inc(turned2, 1)
                over_chunks(pe, to_rows, slots=BANKS)

            @block.vector
            def _(dve):
                def measure(c, s, n):
                    q = n // PER
                    dve.wait_ge(turned2, c + 1)
                    for k in range(PER):
                        ins = dve.bn_stats(ln_parts[0:q, s, k, :], ps[0:q, s, k * D:(k + 1) * D])
                    ins.then_inc(ln_stat, 1)

                def aggregate(c, s, n):
                    q = n // PER
                    dve.wait_ge(ln_stat, c + 1)
                    dve.sem_inc(aggregating, 1)
                    for k in range(PER):
                        ins = dve.bn_aggr(ln_out[0:q, s, k, :], ln_parts[0:q, s, k, :])
                    ins.then_inc(measured, 1)

                def invert_and_shift(c, s, n):
                    q = n // PER
                    dve.wait_ge(rooted, c + 1)
                    dve.reciprocal(ln_rstd[0:q, s, 0, :], ln_root[0:q, s, :]).then_inc(ln_inverse, 1)
                    dve.wait_ge(ln_inverse, c + 1)
                    dve.scalar_tensor_tensor(ln_rstd[0:q, s, 1, :], ln_out[0:q, s, :, 0], -1.0, ln_rstd[0:q, s, 0, :],
                                             ALU.mult, ALU.mult).then_inc(ln_ready, 1)

                def normalize(c, s, n):
                    if s % 2 == 0:
                        return
                    q = n // PER
                    dve.wait_ge(ln_ready, c + 1)
                    dve.wait_ge(out_done[s % 4], uses(c, s % 4, 4) + 16)
                    for k in range(PER):
                        ins = dve.tensor_scalar(staged_out[0:q, s % 4, k * D:(k + 1) * D],
                                                ps[0:q, s, k * D:(k + 1) * D], ln_rstd[0:q, s, 0, k:k + 1],
                                                ln_rstd[0:q, s, 1, k:k + 1], ALU.mult, ALU.add)
                    ins.then_inc(normed[1], 2)

                lagging(dve, [measure, aggregate, between, between, invert_and_shift, normalize], BANKS)

            @block.scalar
            def _(act):
                def relu(c, s, n):
                    wait(act, residual, c - 3)
                    act.activation(staged_relu[:, s % 4, 0:n], y2[:, bass.ds(c * CHUNK, n)], ACT.Relu,
                                   bias=bn_col[:, 1, 3:4], scale=bn_col[:, 1, 1:2]).then_inc(relu2, 1)

                def root(c, s, n):
                    q = n // PER
                    act.wait_ge(measured, c + 1)
                    act.activation(ln_root[0:q, s, :], ln_out[0:q, s, :, 1], ACT.Sqrt, bias=eps[0:q, :]
                                   ).then_inc(rooted, 1)

                def normalize(c, s, n):
                    if s % 2:
                        return
                    q = n // PER
                    act.wait_ge(ln_ready, c + 1)
                    act.wait_ge(out_done[s % 4], uses(c, s % 4, 4) + 16)
                    for k in range(PER):
                        ins = act.activation(staged_out[0:q, s % 4, k * D:(k + 1) * D], ps[0:q, s, k * D:(k + 1) * D],
                                             ACT.Identity, bias=ln_rstd[0:q, s, 1, k:k + 1],
                                             scale=ln_rstd[0:q, s, 0, k:k + 1])
                    ins.then_inc(normed[0], 2)
                lagging(act, [relu] + 3 * [between] + [root] + 2 * [between] + [normalize], BANKS)


def kernel(x, src, dst, edge_attr_16, L0_gnn_ee_w1, L0_gnn_ee_b1, L0_gnn_ee_g1, L0_gnn_ee_bb1, L0_gnn_ee_w2,
           L0_gnn_ee_b2, L0_gnn_mlp_w1, L0_gnn_mlp_b1, L0_gnn_mlp_g1, L0_gnn_mlp_bb1, L0_gnn_mlp_w2,
           L0_gnn_mlp_b2, L0_gnn_mlp_g2, L0_gnn_mlp_bb2):
    import concourse.bacc as bacc
    from concourse.bass_utils import run_bass_kernel_spmd

    def laid(v):
        return np.ascontiguousarray(v)

    padded = TILES * P
    x, src, dst, edges = (np.asarray(v) for v in (x, src, dst, edge_attr_16))
    src_p = np.zeros(padded, src.dtype)
    src_p[:E] = src
    dst_p = np.full(padded, NO_NODE, dst.dtype)
    dst_p[:E] = dst
    edges_p = np.zeros((padded, ED), edges.dtype)
    edges_p[:E] = edges
    w1 = np.asarray(L0_gnn_ee_w1)
    w1bd = np.zeros((PARTS, PAIR, ED, PAIR, D), w1.dtype)
    for q in range(PAIR):
        w1bd[:, q, :, q] = w1
    low = np.zeros((PARTS, PAIR * ED, 2), np.float32)
    low[1::2, :, 0] = 1.0
    low[2:, :, 1] = 1.0
    eye = np.eye(P, dtype=np.float32)
    arrays = {
        "x": laid(x), "x_t": laid(x.T),
        "src_tiles": laid(src_p.reshape(TILES, P).T), "dst_tiles": laid(dst_p.reshape(TILES, P).T),
        "dst_groups": laid(dst_p.reshape(GROUPS, GROUP_EDGES)),
        "edges": laid(edges_p.reshape(P, TILES * ED)),
        "edges_t": laid(edges_p.reshape(TILES // PAIR, PAIR, P, ED).transpose(1, 3, 0, 2)
                        .reshape(PAIR * ED, TILES // PAIR * P)),
        "ee_w1bd": laid(w1bd.reshape(P, PAIR * D)), "low_rows": laid(low.reshape(P, 2)),
        "ee_w1": laid(w1), "ee_w2": laid(L0_gnn_ee_w2),
        "mlp_w1": laid(L0_gnn_mlp_w1), "mlp_w2": laid(L0_gnn_mlp_w2),
        "ee_b1": laid(L0_gnn_ee_b1), "ee_g1": laid(L0_gnn_ee_g1), "ee_bb1": laid(L0_gnn_ee_bb1),
        "ee_b2": laid(L0_gnn_ee_b2), "mlp_b1": laid(L0_gnn_mlp_b1), "mlp_g1": laid(L0_gnn_mlp_g1),
        "mlp_bb1": laid(L0_gnn_mlp_bb1), "mlp_b2": laid(L0_gnn_mlp_b2), "mlp_g2": laid(L0_gnn_mlp_g2),
        "mlp_bb2": laid(L0_gnn_mlp_bb2),
        "ident": eye, "iota": laid(np.tile(np.arange(WINDOW, dtype=np.float32), (P, 1))),
        "block_mask": laid(np.kron(np.eye(P // ED, dtype=np.float32), np.ones((ED, ED), np.float32))),
        "fold": laid(np.tile(np.eye(ED, dtype=np.float32), (P // ED, 1))),
    }
    nc = bacc.Bacc("TRN2", target_bir_lowering=False, num_devices=1)
    aps = {n: nc.dram_tensor(f"in_{n}", v.shape, mybir.dt.from_np(v.dtype), kind="ExternalInput").ap()
           for n, v in arrays.items()}
    aps["out"] = nc.dram_tensor("out_0", (N, D), F32, kind="ExternalOutput").ap()
    build(nc, aps)
    r = run_bass_kernel_spmd(nc, [{f"in_{n}": v for n, v in arrays.items()}], core_ids=[0])
    return r.results[0]["out_0"]
```
